# Optimizing a Trainium2 kernel written in Bass

```python
import numpy as np
import jax
import jax.numpy as jnp

def _softmax(x, axis=-1):
    return jax.nn.softmax(x, axis=axis)

def _gelu(x):
    return jax.nn.gelu(x, approximate=True)

def _silu(x):
    return jax.nn.silu(x)

def _sigmoid(x):
    return jax.nn.sigmoid(x)

def _layernorm(x, axis=-1, eps=1e-05):
    m = jnp.mean(x, axis=axis, keepdims=True)
    v = jnp.var(x, axis=axis, keepdims=True)
    return (x - m) / jnp.sqrt(v + eps)

def _scatter_add(tgt, idx, src, axis=0):
    return tgt.at[idx].add(src)

def _segment_sum(src, seg, n):
    return jax.ops.segment_sum(src, seg, n)
kernel_name = 'mk_macaron_d1_jaxref_r4_9908c7'

def setup_inputs(seed: int=0):
    np.random.seed(seed)
    _w = jnp.asarray

    def _L0_attn_setup():
        import jax, jax.numpy as jnp
        import numpy as np
        D_MODEL = 256
        EXPAND = 2
        E = EXPAND * D_MODEL
        N_STATE = 16
        DT_RANK = 64
        K = 4
        B_SZ, L = (4, 1024)
        key = jax.random.key(seed)
        ks = jax.random.split(key, 10)
        s = lambda *sh: 1.0 / np.sqrt(sh[0])
        inp = {'x': jax.random.normal(ks[0], (B_SZ, L, D_MODEL), jnp.float32), 'w_in': jax.random.normal(ks[1], (D_MODEL, 2 * E), jnp.float32) * s(D_MODEL), 'w_conv': jax.random.normal(ks[2], (E, 1, K), jnp.float32) * s(K), 'b_conv': jax.random.normal(ks[3], (E,), jnp.float32) * 0.01, 'w_sel': jax.random.normal(ks[4], (E, 2 * N_STATE + DT_RANK), jnp.float32) * s(E), 'w_dt': jax.random.normal(ks[5], (DT_RANK, E), jnp.float32) * s(DT_RANK), 'b_dt': jax.random.normal(ks[6], (E,), jnp.float32) * 0.01, 'w_out': jax.random.normal(ks[7], (E, D_MODEL), jnp.float32) * s(E)}
        p = np.sqrt(1 + 2 * np.arange(E, dtype=np.float32))
        A = np.tril(p[:, None] * p[None, :]) - np.diag(np.arange(E, dtype=np.float32))
        inp['A'] = jnp.asarray(-A)
        inp['Dp'] = jnp.ones((E,), jnp.float32)
        return inp
    _L0_attn_in = _L0_attn_setup()

    def _L0_ffn_setup():
        import jax, jax.numpy as jnp
        import numpy as np
        B, S, D = (2, 512, 256)
        I = 128
        E = 16
        TOP_K = 2

        def _mlp(x, wg, wu, wd):
            return jnp.einsum('bsi,id->bsd', jax.nn.silu(x @ wg) * (x @ wu), wd)
        key = jax.random.key(seed)
        ks = jax.random.split(key, 10)
        sc_d = 1.0 / np.sqrt(D)
        sc_i = 1.0 / np.sqrt(I)
        return {'x': jax.random.normal(ks[0], (B, S, D), dtype=jnp.float32), 'gate_w': jax.random.normal(ks[1], (D, E), dtype=jnp.float32) * sc_d, 'gate_b': jnp.zeros((E,), dtype=jnp.float32), 'shared_wg': jax.random.normal(ks[2], (D, I), dtype=jnp.float32) * sc_d, 'shared_wu': jax.random.normal(ks[3], (D, I), dtype=jnp.float32) * sc_d, 'shared_wd': jax.random.normal(ks[4], (I, D), dtype=jnp.float32) * sc_i, 'experts_wg': jax.random.normal(ks[5], (E, D, I), dtype=jnp.float32) * sc_d, 'experts_wu': jax.random.normal(ks[6], (E, D, I), dtype=jnp.float32) * sc_d, 'experts_wd': jax.random.normal(ks[7], (E, I, D), dtype=jnp.float32) * sc_i}
    _L0_ffn_in = _L0_ffn_setup()
    _d = {'L0_attn_x': _L0_attn_in['x'], 'L0_attn_w_in': _L0_attn_in['w_in'], 'L0_attn_w_conv': _L0_attn_in['w_conv'], 'L0_attn_b_conv': _L0_attn_in['b_conv'], 'L0_attn_w_sel': _L0_attn_in['w_sel'], 'L0_attn_w_dt': _L0_attn_in['w_dt'], 'L0_attn_b_dt': _L0_attn_in['b_dt'], 'L0_attn_w_out': _L0_attn_in['w_out'], 'L0_attn_A': _L0_attn_in['A'], 'L0_attn_Dp': _L0_attn_in['Dp'], 'L0_ffn_gate_w': _L0_ffn_in['gate_w'], 'L0_ffn_gate_b': _L0_ffn_in['gate_b'], 'L0_ffn_shared_wg': _L0_ffn_in['shared_wg'], 'L0_ffn_shared_wu': _L0_ffn_in['shared_wu'], 'L0_ffn_shared_wd': _L0_ffn_in['shared_wd'], 'L0_ffn_experts_wg': _L0_ffn_in['experts_wg'], 'L0_ffn_experts_wu': _L0_ffn_in['experts_wu'], 'L0_ffn_experts_wd': _L0_ffn_in['experts_wd']}
    _x0 = _d['L0_attn_x']
    _d['L0_attn_x'] = jax.random.normal(jax.random.fold_in(jax.random.key(seed), 1), (8, 1024, 256), dtype=_x0.dtype)
    del _x0
    return _d

def reference(L0_attn_x, L0_attn_w_in, L0_attn_w_conv, L0_attn_b_conv, L0_attn_w_sel, L0_attn_w_dt, L0_attn_b_dt, L0_attn_w_out, L0_attn_A, L0_attn_Dp, L0_ffn_gate_w, L0_ffn_gate_b, L0_ffn_shared_wg, L0_ffn_shared_wu, L0_ffn_shared_wd, L0_ffn_experts_wg, L0_ffn_experts_wu, L0_ffn_experts_wd):

    def _L0_attn_ref(x, w_in, w_conv, b_conv, w_sel, w_dt, b_dt, w_out, A, Dp):
        import jax, jax.numpy as jnp
        import numpy as np
        D_MODEL = 256
        EXPAND = 2
        E = EXPAND * D_MODEL
        N_STATE = 16
        DT_RANK = 64
        K = 4
        B_SZ, L = (4, 1024)
        xz = x @ w_in
        xc, z = jnp.split(xz, 2, axis=-1)
        xt = jnp.transpose(xc, (0, 2, 1))
        conv = jax.lax.conv_general_dilated(xt, w_conv, window_strides=(1,), padding=[(K - 1, 0)], feature_group_count=E, dimension_numbers=('NCH', 'OIH', 'NCH')) + b_conv[None, :, None]
        xa = jax.nn.silu(jnp.transpose(conv, (0, 2, 1)))
        bcd = xa @ w_sel
        Bm, Cm, delta = jnp.split(bcd, [N_STATE, 2 * N_STATE], axis=-1)
        delta = delta @ w_dt + b_dt
        out = xa * jax.nn.silu(z)
        return out @ w_out

    def _L0_ffn_ref(x, gate_w, gate_b, shared_wg, shared_wu, shared_wd, experts_wg, experts_wu, experts_wd):
        import jax, jax.numpy as jnp
        import numpy as np
        B, S, D = (2, 512, 256)
        I = 128
        E = 16
        TOP_K = 2

        def _mlp(x, wg, wu, wd):
            return jnp.einsum('bsi,id->bsd', jax.nn.silu(x @ wg) * (x @ wu), wd)
        router_logits = jax.nn.sigmoid(x @ gate_w + gate_b)
        expert_values, expert_indices = jax.lax.top_k(router_logits, k=TOP_K)
        expert_values = expert_values / jnp.sum(expert_values, axis=-1, keepdims=True)
        hg = jnp.einsum('bsd,edi->bsei', x, experts_wg)
        hu = jnp.einsum('bsd,edi->bsei', x, experts_wu)
        all_outputs = jnp.einsum('bsei,eid->bsed', jax.nn.silu(hg) * hu, experts_wd)
        selected = jnp.take_along_axis(all_outputs, expert_indices[..., None], axis=2)
        expert_weighted = jnp.sum(expert_values[..., None] * selected, axis=2)
        return x + _mlp(x, shared_wg, shared_wu, shared_wd) + expert_weighted
    x = L0_attn_x
    x = x + 0.5 * _L0_ffn_ref(_layernorm(x, axis=-1), L0_ffn_gate_w, L0_ffn_gate_b, L0_ffn_shared_wg, L0_ffn_shared_wu, L0_ffn_shared_wd, L0_ffn_experts_wg, L0_ffn_experts_wu, L0_ffn_experts_wd)
    x = x + _L0_attn_ref(_layernorm(x, axis=-1), L0_attn_w_in, L0_attn_w_conv, L0_attn_b_conv, L0_attn_w_sel, L0_attn_w_dt, L0_attn_b_dt, L0_attn_w_out, L0_attn_A, L0_attn_Dp)
    x = x + 0.5 * _L0_ffn_ref(_layernorm(x, axis=-1), L0_ffn_gate_w, L0_ffn_gate_b, L0_ffn_shared_wg, L0_ffn_shared_wu, L0_ffn_shared_wd, L0_ffn_experts_wg, L0_ffn_experts_wu, L0_ffn_experts_wd)
    return x

_drawn_inputs = setup_inputs


def setup_inputs(seed=0):
    import zlib

    import numpy as np

    out = dict(_drawn_inputs(seed))
    spreads = {'L0_attn_Dp': (1.0, 0.2), 'L0_ffn_gate_b': (0.0, 0.1)}
    factors = {'L0_attn_b_conv': 21.496}
    for name, (base, spread) in spreads.items():
        noise = np.random.default_rng([zlib.crc32(name.encode()), seed]).standard_normal(out[name].shape)
        drawn = base * np.exp(spread * noise) if base else spread * noise
        out[name] = jnp.asarray(drawn.astype(out[name].dtype))
    for name, factor in factors.items():
        out[name] = (out[name] * factor).astype(out[name].dtype)
    return out
```

```python
from contextlib import ExitStack

import concourse.bass as bass
from concourse import mybir
from concourse.alu_op_type import AluOpType as ALU

ACT = mybir.ActivationFunctionType
AX = mybir.AxisListType
F32 = mybir.dt.float32
F32R = mybir.dt.float32r
BF16 = mybir.dt.bfloat16
I32 = mybir.dt.int32
U32 = mybir.dt.uint32

P = 128
G = 4
GT = G * P
EPS = 1e-5
SATURATED = 17.33


def wait(engine, semaphore, value):
    if not (isinstance(value, int) and value <= 0):
        engine.wait_ge(semaphore, value)


def build_macaron(nc, x, w_in, w_conv, b_conv, w_out, gate_w, gate_b, shared_wg, shared_wu, shared_wd,
                  experts_wg, experts_wu, experts_wd, out):
    B, L, D = x.shape
    T = B * L
    E, _, H = experts_wg.shape
    M = w_out.shape[0]
    TAPS = w_conv.shape[2]
    K = 2
    KC = D // P
    FC = M // P
    NT = T // P
    NG = T // GT
    NP = NG // 2
    HU = 2 * H
    TILES = -(-(T * K // P + E - 1) // 2) * 2
    COLS = T // P
    assert D == 256 and H == P and L == 2 * GT and M == FC * P and TILES <= 2 * P

    x_rows = x.rearrange("b l d -> (b l) d")
    out_rows = out.rearrange("b l d -> (b l) d")

    def grouped(rows):
        return rows.rearrange("(i p) d -> p i d", p=P)

    normed = [nc.dram_tensor(f"normed{f}", (T, D), F32).ap() for f in range(2)]
    sums = [nc.dram_tensor(f"sums{f}", (T, D), F32).ap() for f in range(2)]
    expert_out = [nc.dram_tensor(f"expert_out{f}", (TILES * P, D), F32).ap() for f in range(2)]
    lists = [nc.dram_tensor(f"lists{f}", (P * E * COLS, 1), I32).ap() for f in range(2)]
    tables = [nc.dram_tensor(f"tables{f}", (P, 4), I32).ap() for f in range(2)]

    with ExitStack() as ctx:
        def sb(name, shape, dt=F32):
            return ctx.enter_context(nc.sbuf_tensor(name, shape, dt))

        def sem(name):
            return ctx.enter_context(nc.semaphore(name))

        def parts(name, shape):
            return sb(name + "_hi", shape, F32R), sb(name + "_lo", shape, F32R)

        gate = parts("gate", [P, KC * E])
        up_s = parts("up_s", [P, KC * HU])
        down_s = parts("down_s", [P, D])
        up_e = parts("up_e", [P, E * KC * HU])
        down_e = parts("down_e", [P, E * D])
        win = parts("win", [P, KC * 2 * M])
        wout = parts("wout", [P, FC * D])
        taps = sb("taps", [P, FC, TAPS])
        conv_bias = sb("conv_bias", [P, FC])
        gate_bias = sb("gate_bias", [P, E])

        ident = sb("ident", [P, P])
        before = sb("before", [P, P], BF16)
        ones = sb("ones", [P, P], BF16)
        expert_ids = sb("expert_ids", [P, E])
        tile_ids = sb("tile_ids", [P, 2])
        ones_e = sb("ones_e", [P, E])
        minus_half = sb("minus_half", [P, G])
        token_ids = sb("token_ids", [P, NT], I32)

        rows = [sb(f"rows{b}", [P, G, D]) for b in range(2)]
        norm = [sb(f"norm{b}", [P, G, D]) for b in range(2)]
        base = [sb(f"base{b}", [P, G, D]) for b in range(2)]
        xt_hi = sb("xt_hi", [P, KC * GT], F32R)
        xt_lo = sb("xt_lo", [P, KC * GT], F32R)
        silu_g = sb("silu_g", [P, GT])
        hid = sb("hid", [P, GT])
        hid_hi = sb("hid_hi", [P, GT], F32R)
        hid_lo = sb("hid_lo", [P, GT], F32R)
        picked = sb("picked", [P, G, K, D])
        xc = [sb(f"xc{i}", [P, GT + TAPS - 1]) for i in range(2)]
        halo = sb("halo", [P, FC, TAPS - 1])
        silu_z = [sb(f"silu_z{i}", [P, GT]) for i in range(2)]
        conv = [sb(f"conv{i}", [P, GT]) for i in range(2)]
        mix_hi = [sb(f"mix_hi{i}", [P, GT], F32R) for i in range(2)]
        mix_lo = [sb(f"mix_lo{i}", [P, GT], F32R) for i in range(2)]

        stats = sb("stats", [P, G, 6])
        mean_var = sb("mean_var", [P, G, 2])
        var_eps = sb("var_eps", [P, G])
        rstd = sb("rstd", [P, G])
        logit = sb("logit", [P, G, E])
        best = sb("best", [P, G, 8])
        best_at = sb("best_at", [P, G, 8], U32)
        chosen = sb("chosen", [P, G * K])
        onehot = sb("onehot", [P, G * K, E])
        members = sb("members", [P, G, E], BF16)
        rank_all = sb("rank_all", [P, G, E])
        rank_pick = sb("rank_pick", [P, G * K, E])
        rank = sb("rank", [P, G * K])
        rank_i = sb("rank_i", [P, G * K], I32)
        slot_row = sb("slot_row", [P, G * K], I32)
        slot_col = sb("slot_col", [P, G * K], I32)
        slot_ec = sb("slot_ec", [P, G * K])
        slot = [sb(f"slot{b}", [P, G * K], U32) for b in range(2)]
        token = [sb(f"token{b}", [P, G], I32) for b in range(2)]
        counts = sb("counts", [P, 2, E])
        expert_of = sb("expert_of", [P, NT * K])
        rank_of = sb("rank_of", [P, NT * K])
        logit_of = sb("logit_of", [P, NT * K])
        position = sb("position", [P, NT * K], I32)
        weight = sb("weight", [P, NT, K])
        exp_neg = logit_of[:].rearrange("p (t k) -> p t k", k=K)
        denom = sb("denom", [P, NT])
        tiles_i = sb("tiles_i", [P, E], I32)
        tiles_f = sb("tiles_f", [P, E])
        tiles_upto = sb("tiles_upto", [P, E])
        first_row = sb("first_row", [P, E])
        passed = sb("passed", [P, 2, E])
        passed_n = sb("passed_n", [P, 2, E])
        tab_e = sb("tab_e", [P, 2])
        tab_s = sb("tab_s", [P, 2])
        tab_i = sb("tab_i", [P, 2, 2], I32)
        tab_row = sb("tab_row", [1, 2 * TILES], I32)
        list_sb = sb("list_sb", [P, E * COLS], I32)
        gather_at = sb("gather_at", [P, 4], U32)
        weight_now = sb("weight_now", [P, G * K])
        pick_at = sb("pick_at", [P, G * K], U32)

        pT = ctx.enter_context(nc.psum_tensor("pT", [P, 2, 512], F32))
        pU = ctx.enter_context(nc.psum_tensor("pU", [P, 2, 512], F32))
        pV = ctx.enter_context(nc.psum_tensor("pV", [P, 2, 512], F32))
        pO = ctx.enter_context(nc.psum_tensor("pO", [P, 2, 512], F32))
        p_gate = pV[:, 0, 0:G * E].rearrange("p (i e) -> p i e", i=G)
        p_rank = pV[:, 1, 0:G * E].rearrange("p (i e) -> p i e", i=G)
        p_total = pV[:, 1, G * E:G * E + E]

        tile_in = [norm[0][:, i, :] for i in range(4)]
        tile_hi = [xt_hi[:, c * D:(c + 1) * D] for c in range(2)]
        tile_lo = [xt_lo[:, c * D:(c + 1) * D] for c in range(2)]
        tile_silu = [silu_g[:, c * H:(c + 1) * H] for c in range(2)]
        tile_hid = [hid[:, c * H:(c + 1) * H] for c in range(2)]
        tile_hid_hi = [hid_hi[:, c * P:(c + 1) * P] for c in range(2)]
        tile_hid_lo = [hid_lo[:, c * P:(c + 1) * P] for c in range(2)]
        tile_out = [base[0][:, i, :] for i in range(4)]

        stage = [picked[:, 2 * i:2 * i + 2, :, :].rearrange("p i k d -> p (i k d)") for i in range(2)]
        loads = []

        def piece(pair, at, cols, scale, *sources):
            loads.append((pair, at, cols, scale, sources))

        ew = 4
        piece(gate, 0, KC * E, 1.0, (0, E, E, gate_w.rearrange("(k p) e -> p k e", p=P)))
        piece(up_s, 0, KC * HU, 1.0, (0, H, HU, shared_wg.rearrange("(k p) h -> p k h", p=P)),
              (H, H, HU, shared_wu.rearrange("(k p) h -> p k h", p=P)))
        piece(down_s, 0, D, 0.5, (0, D, D, shared_wd.rearrange("(k p) d -> p k d", p=P)))
        LOADS_A = len(loads)
        g_view = experts_wg.rearrange("e (k p) h -> p (e k) h", p=P)
        u_view = experts_wu.rearrange("e (k p) h -> p (e k) h", p=P)
        d_view = experts_wd.rearrange("e h d -> h e d")
        for e in range(0, E, 2):
            piece(up_e, e * KC * HU, 2 * KC * HU, 1.0, (0, H, HU, g_view[:, e * KC:(e + 2) * KC, :]),
                  (H, H, HU, u_view[:, e * KC:(e + 2) * KC, :]))
        for e in range(0, E, ew):
            piece(down_e, e * D, ew * D, 0.5, (0, D, D, d_view[:, e:e + ew, :]))
        LOADS_C = len(loads)
        win_view = w_in.rearrange("(k p) m -> p k m", p=P)
        for k in range(KC):
            piece(win, k * 2 * M, 2 * M, 1.0, (0, 2 * M, 2 * M, win_view[:, k:k + 1, :]))
        piece(wout, 0, FC * D, 1.0, (0, D, D, w_out.rearrange("(f p) d -> p f d", p=P)))
        loaded = {0: 0, 1: 0}
        load_ready = []
        for i, (_, _, _, _, sources) in enumerate(loads):
            loaded[i % 2] += 16 * len(sources)
            load_ready.append(loaded[i % 2])

        s_const = sem("s_const")
        s_zero = sem("s_zero")
        s_small = sem("s_small")
        s_cleared = sem("s_cleared")
        s_stage = [sem("s_stage0"), sem("s_stage1")]
        s_whi = sem("s_whi")
        s_wlo = sem("s_wlo")
        s_passed_pool = sem("s_passed_pool")
        s_passed_dve = sem("s_passed_dve")
        s_rows = [sem("s_rows0"), sem("s_rows1")]
        s_stats = sem("s_stats")
        s_aggr = sem("s_aggr")
        s_vareps = sem("s_vareps")
        s_rstd = sem("s_rstd")
        s_norm = sem("s_norm")
        s_half = sem("s_half")
        s_base = sem("s_base")
        s_xt = sem("s_xt")
        s_xthi = sem("s_xthi")
        s_xtlo = sem("s_xtlo")
        s_gate = sem("s_gate")
        s_up = sem("s_up")
        s_silu = sem("s_silu")
        s_hid = sem("s_hid")
        s_hidhi = sem("s_hidhi")
        s_hidlo = sem("s_hidlo")
        s_down = sem("s_down")
        s_sum = sem("s_sum")
        s_route = sem("s_route")
        s_members = sem("s_members")
        s_rank = sem("s_rank")
        s_ranked = sem("s_ranked")
        s_slot = sem("s_slot")
        s_token = sem("s_token")
        s_scat = [sem("s_scat0"), sem("s_scat1")]
        s_normed = [sem("s_normed0"), sem("s_normed1")]
        s_sums = [sem("s_sums0"), sem("s_sums1")]
        s_plan = sem("s_plan")
        s_tab = sem("s_tab")
        s_tabd = sem("s_tabd")
        s_lists = sem("s_lists")
        s_logits = sem("s_logits")
        s_exp = sem("s_exp")
        s_pos = sem("s_pos")
        c_at = sem("c_at")
        c_in = [sem(f"c_in{i}") for i in range(4)]
        c_xt = sem("c_xt")
        c_hi = sem("c_hi")
        c_lo = sem("c_lo")
        c_up = sem("c_up")
        c_silu = sem("c_silu")
        c_hid = sem("c_hid")
        c_ht = sem("c_ht")
        c_hidhi = sem("c_hidhi")
        c_hidlo = sem("c_hidlo")
        c_down = sem("c_down")
        c_out = sem("c_out")
        c_stored = [sem(f"c_stored{i}") for i in range(4)]
        m_at = sem("m_at")
        m_picked = sem("m_picked")
        m_add = sem("m_add")
        m_comb = sem("m_comb")
        m_win = sem("m_win")
        m_xc = sem("m_xc")
        m_halo = sem("m_halo")
        m_sz = sem("m_sz")
        m_tap = sem("m_tap")
        m_xa = sem("m_xa")
        m_mix = sem("m_mix")
        m_mixhi = sem("m_mixhi")
        m_mixlo = sem("m_mixlo")
        m_wout = sem("m_wout")
        m_x3 = sem("m_x3")
        s_out = [sem("s_out0"), sem("s_out1")]

        CONSTS = 11
        SCAT = 16 * G * K
        block = ctx.enter_context(nc.Block())

        def split3(a, b):
            return [(a[0], b[0]), (a[0], b[1]), (a[1], b[0])]

        @block.sync
        def _(sp):
            def load_pieces(first, end):
                for i in range(first, end):
                    _, _, cols, _, sources = loads[i]
                    if i >= 2:
                        sp.wait_ge(s_whi, i - 1)
                        sp.wait_ge(s_wlo, i - 1)
                    for at, width, step, src in sources:
                        dst = stage[i % 2][:, 0:cols].rearrange("p (n s) -> p n s", s=step)[:, :, at:at + width]
                        sp.dma_start(dst, src).then_inc(s_stage[i % 2], 16)

            load_pieces(0, LOADS_A)
            sp.dma_start(taps[:], w_conv.rearrange("(f p) o t -> p f (o t)", p=P)).then_inc(s_small, 16)
            with nc.allow_non_contiguous_dma("one small load"):
                sp.dma_start(conv_bias[:], b_conv.rearrange("(f p) -> p f", p=P)).then_inc(s_small, 16)
            sp.dma_start(gate_bias[:], gate_b.partition_broadcast(P)).then_inc(s_small, 16)
            sp.wait_ge(s_const, CONSTS)
            for f in range(2):
                sp.dma_start(lists[f].rearrange("(p c) o -> p (c o)", p=P), list_sb[:]).then_inc(s_cleared, 16)
            load_pieces(LOADS_A, len(loads))

            def load_rows(src, n, b):
                sp.dma_start(rows[b][:], grouped(src[bass.ds(n * GT, GT), :])).then_inc(s_rows[b], 16)

            def store_group(f, n, b):
                g = n - f * NG
                sp.wait_ge(s_norm, n + 1 if f == 0 else NG + 2 * g + 2)
                sp.dma_start(grouped(normed[f][bass.ds(g * GT, GT), :]), norm[b if f == 0 else 1][:])\
                    .then_inc(s_normed[b], 16)
                sp.wait_ge(s_sum, n + 1)
                sp.dma_start(grouped(sums[f][bass.ds(g * GT, GT), :]), base[b][:]).then_inc(s_sums[b], 16)

            def plan(f):
                sp.wait_ge(s_tab, f + 1)
                sp.dma_start(tables[f], tab_i[:].rearrange("p a c -> p (a c)")).then_inc(s_tabd, 16)
                sp.wait_ge(s_tabd, 32 * f + 16)
                if f == 1:
                    sp.wait_ge(c_up, TILES)
                sp.dma_start(tab_row[:], tables[f][0:TILES // 2, :].rearrange("(o p) c -> o (p c)", o=1)).then_inc(s_tabd, 16)
                for b in range(2):
                    sp.wait_ge(s_scat[b], SCAT * NP * (f + 1))
                sp.dma_start(list_sb[:], lists[f].rearrange("(p c) o -> p (c o)", p=P)).then_inc(s_lists, 16)

            def store_tiles(f):
                with sp.Fori(0, TILES // 4) as q:
                    for i in range(4):
                        sp.wait_ge(c_out, f * TILES + q * 4 + i + 1)
                        sp.dma_start(expert_out[f][bass.ds((q * 4 + i) * P, P), :], tile_out[i])\
                            .then_inc(c_stored[i], 16)

            for b in range(2):
                load_rows(x_rows, b, b)
            with sp.Fori(0, NP - 1) as j:
                for b in range(2):
                    n = j * 2 + b
                    store_group(0, n, b)
                    load_rows(x_rows, n + 2, b)
            for b in range(2):
                store_group(0, NG - 2 + b, b)
            plan(0)
            store_tiles(0)
            for b in range(2):
                sp.wait_ge(s_sums[b], 16 * NP)
            for b in range(2):
                load_rows(sums[0], b, b)
            with sp.Fori(0, NP - 1) as j:
                for b in range(2):
                    n = j * 2 + NG + b
                    store_group(1, n, b)
                    load_rows(sums[0], n - NG + 2, b)
            for b in range(2):
                store_group(1, 2 * NG - 2 + b, b)
            plan(1)
            store_tiles(1)
            for b in range(2):
                sp.wait_ge(s_sums[b], 32 * NP)
            for b in range(2):
                load_rows(sums[1], b, b)
            def store_out(g, j, b):
                sp.wait_ge(m_comb, NG + g + 1)
                sp.dma_start(grouped(out_rows[bass.ds(g * GT, GT), :]), rows[b][:]).then_inc(s_out[b], 16)
                sp.wait_ge(s_out[b], (j + 1) * 16)

            with sp.Fori(0, NP - 1) as j:
                for b in range(2):
                    g = j * 2 + b
                    store_out(g, j, b)
                    load_rows(sums[1], g + 2, b)
            for b in range(2):
                store_out(NG - 2 + b, NP - 1, b)

        def all_groups(engine, body):
            for b in range(2):
                body(b, 0, b)
            with engine.Fori(1, NP - 1) as j:
                for b in range(2):
                    body(j * 2 + b, j, b)
            for b in range(2):
                body(NG - 2 + b, NP - 1, b)

        def all_tiles(engine, body):
            for i in range(4):
                body(i, 0, i)
            with engine.Fori(1, TILES // 4) as q:
                for i in range(4):
                    body(q * 4 + i, q, i)
            for i in range(3):
                body(TILES + i, TILES // 4, i)

        def in_range(t):
            return not isinstance(t, int) or 0 <= t < TILES

        @block.gpsimd
        def _(pool):
            pool.memset(ident[:], 0.0).then_inc(s_const, 1)
            pool.memset(before[:], 1.0).then_inc(s_const, 1)
            pool.memset(ones[:], 1.0).then_inc(s_const, 1)
            pool.memset(ones_e[:], 1.0).then_inc(s_const, 1)
            pool.memset(minus_half[:], -0.5).then_inc(s_const, 1)
            pool.memset(list_sb[:], 0).then_inc(s_const, 1)
            pool.iota(expert_ids[:], [[1, E]], base=0, channel_multiplier=0,
                      allow_small_or_imprecise_dtypes=True).then_inc(s_const, 1)
            pool.iota(tile_ids[:], [[1, 2]], base=0, channel_multiplier=2,
                      allow_small_or_imprecise_dtypes=True).then_inc(s_const, 1)
            pool.iota(token_ids[:], [[P, NT]], base=0, channel_multiplier=1).then_inc(s_const, 1)
            pool.wait_ge(s_const, 9)
            pool.affine_select(out=ident[:], in_=ident[:], compare_op=ALU.not_equal, fill=1.0, base=0,
                               pattern=[[-1, P]], channel_multiplier=1).then_inc(s_const, 1)
            pool.affine_select(out=before[:], in_=before[:], compare_op=ALU.is_gt, fill=0.0, base=0,
                               pattern=[[1, P]], channel_multiplier=-1).then_inc(s_const, 1)
            pool.wait_ge(s_cleared, 32)

            def inverse_std(m):
                pool.wait_ge(s_vareps, m + 1)
                pool.tensor_tensor(rstd[:], var_eps[:], minus_half[:], ALU.pow).then_inc(s_rstd, 1)

            def make_base(n, j, b, src):
                wait(pool, s_sums[b], j * 16)
                pool.sem_inc(s_passed_pool, 1)
                pool.tensor_scalar(base[b][:], src[:], 0.5, None, ALU.mult).then_inc(s_half, 1)
                pool.wait_ge(s_half, n + 1)
                pool.tensor_tensor(base[b][:], base[b][:], rows[b][:], ALU.add).then_inc(s_base, 1)

            def scatter(f, n, b):
                pool.wait_ge(s_slot, n + 1)
                pool.tensor_copy(token[b][:], token_ids[:, bass.ds((n - f * NG) * G, G)]).then_inc(s_token, 1)
                pool.wait_ge(s_token, n + 1)
                pool.sem_inc(s_passed_pool, 1)
                for c in range(G * K):
                    pool.indirect_dma_start(lists[f], bass.IndirectOffsetOnAxis(slot[b][:, c:c + 1], 0),
                                            token[b][:, c // K:c // K + 1], None).then_inc(s_scat[b], 16)

            def route_groups(g, j, b):
                inverse_std(g)
                pool.wait_ge(s_norm, g + 1)
                make_base(g, j, b, norm[b])
                scatter(0, g, b)

            def gather_tiles(f):
                for b in range(2):
                    pool.wait_ge(s_normed[b], 16 * NP * (f + 1))
                pool.wait_ge(s_xt, NG * (1 + 2 * f))
                pool.wait_ge(s_tabd, 32 * (f + 1))
                pool.wait_ge(s_lists, 16 * (f + 1))

                def gather(t, q, i):
                    if not in_range(t):
                        return
                    wait(pool, c_xt, f * TILES + t - 3)
                    col = pool.value_load(tab_row[0:1, bass.ds((q * 2 + i // 2) * 4 + 2 + i % 2, 1)],
                                          min_val=0, max_val=E * COLS - 1)
                    pool.tensor_copy(gather_at[:, i:i + 1], list_sb[:, bass.ds(col, 1)]).then_inc(c_at, 1)
                    pool.wait_ge(c_at, f * TILES + t + 1)
                    pool.sem_inc(s_passed_pool, 1)
                    pool.indirect_dma_start(tile_in[i], None, normed[f],
                                            bass.IndirectOffsetOnAxis(gather_at[:, i:i + 1], 0))\
                        .then_inc(c_in[i], 16)

                all_tiles(pool, gather)

            def pick(f, g):
                wait(pool, m_comb, f * NG + g)
                pool.tensor_copy(pick_at[:], position[:, bass.ds(g * G * K, G * K)]).then_inc(m_at, 1)
                pool.wait_ge(m_at, f * NG + g + 1)
                pool.sem_inc(s_passed_pool, 1)
                for c in range(G * K):
                    pool.indirect_dma_start(picked[:, c // K, c % K, :], None, expert_out[f],
                                            bass.IndirectOffsetOnAxis(pick_at[:, c:c + 1], 0))\
                        .then_inc(m_picked, 16)

            def wait_experts(f):
                pool.wait_ge(s_pos, f + 1)
                for i in range(4):
                    pool.wait_ge(c_stored[i], 16 * (TILES // 4) * (f + 1))

            def mix_groups(g, j, b):
                inverse_std(g * 2 + NG)
                if not (isinstance(g, int) and g == NG - 1):
                    pick(0, g + 1)
                inverse_std(g * 2 + NG + 1)
                pool.wait_ge(s_norm, g * 2 + NG + 2)
                make_base(g + NG, j + NP, b, norm[1])
                scatter(1, g + NG, b)

            all_groups(pool, route_groups)
            gather_tiles(0)
            wait_experts(0)
            pool.wait_ge(s_whi, len(loads))
            pool.wait_ge(s_wlo, len(loads))
            pick(0, 0)
            all_groups(pool, mix_groups)
            gather_tiles(1)
            wait_experts(1)
            with pool.Fori(0, NG) as g:
                pick(1, g)

        @block.scalar
        def _(act):
            for i, (pair, at, cols, scale, _) in enumerate(loads):
                act.wait_ge(s_stage[i % 2], load_ready[i])
                act.activation(pair[0][:, at:at + cols], stage[i % 2][:, 0:cols], ACT.Copy, scale=scale)\
                   .then_inc(s_whi, 1)

            def x_high(m):
                act.wait_ge(s_xt, m + 1)
                for k in range(KC):
                    last = act.activation(xt_hi[:, k * GT:(k + 1) * GT], pT[:, k, :], ACT.Copy)
                last.then_inc(s_xthi, 1)

            def shared_expert(n):
                act.wait_ge(s_up, n + 1)
                wait(act, s_hid, n)
                act.activation(silu_g[:], pU[:, 0, :], ACT.Silu).then_inc(s_silu, 1)
                act.wait_ge(s_hid, n + 1)
                wait(act, s_down, n)
                act.activation(hid_hi[:], hid[:], ACT.Copy).then_inc(s_hidhi, 1)

            def route_groups(g, j, b):
                wait(act, s_up, g)
                x_high(g)
                shared_expert(g)

            def tiles(f):
                act.wait_ge(s_logits, f + 1)
                act.activation(logit_of[:], logit_of[:], ACT.Exp, scale=-1.0)\
                   .then_inc(s_exp, 1)
                act.wait_ge(s_down, NG * (f + 1))
                act.wait_ge(s_hid, NG * (f + 1))
                act.wait_ge(s_sums[0], 16 * NP * (f + 1))

                def step(u, q, i):
                    done = f * TILES
                    if in_range(u):
                        act.wait_ge(c_xt, done + u + 1)
                        wait(act, c_up, done + u - 1)
                        act.activation(tile_hi[i % 2], pT[:, i % 2, 0:D], ACT.Copy).then_inc(c_hi, 1)
                    t = u - 1
                    if in_range(t):
                        act.wait_ge(c_up, done + t + 1)
                        wait(act, c_hid, done + t - 1)
                        act.activation(tile_silu[(i - 1) % 2], pU[:, (i - 1) % 2, 0:H], ACT.Silu)\
                           .then_inc(c_silu, 1)
                    t = u - 2
                    if in_range(t):
                        act.wait_ge(c_ht, done + t + 1)
                        wait(act, c_down, done + t - 1)
                        act.activation(tile_hid_hi[i % 2], pV[:, i % 2, 0:P], ACT.Copy).then_inc(c_hidhi, 1)
                    t = u - 3
                    if in_range(t):
                        act.wait_ge(c_down, done + t + 1)
                        o = (i - 3) % 4
                        wait(act, c_stored[o], (f * (TILES // 4) + (q if i == 3 else q - 1)) * 16)
                        act.activation(tile_out[o], pO[:, (i - 3) % 2, 0:D], ACT.Copy).then_inc(c_out, 1)

                all_tiles(act, step)

            def mix_groups(g, j, b):
                act.wait_ge(s_up, g + NG)
                x_high(g * 2 + NG)
                for f in range(FC + 1):
                    if f < FC:
                        w = (pU, pV)[f % 2]
                        c = g * FC + f
                        act.wait_ge(m_win, c + 1)
                        wait(act, m_tap, (c - 1) * TAPS)
                        act.activation(xc[f % 2][:, TAPS - 1:], w[:, 0, :], ACT.Copy).then_inc(m_xc, 1)
                        wait(act, m_mix, c - 1)
                        act.activation(silu_z[f % 2][:], w[:, 1, :], ACT.Silu).then_inc(m_sz, 1)
                    if f > 0:
                        c = g * FC + f - 1
                        i = (f - 1) % 2
                        act.wait_ge(m_tap, (c + 1) * TAPS)
                        act.activation(conv[i][:], conv[i][:], ACT.Silu).then_inc(m_xa, 1)
                        act.wait_ge(m_mix, c + 1)
                        wait(act, m_wout, c - 1)
                        act.activation(mix_hi[i][:], conv[i][:], ACT.Copy).then_inc(m_mixhi, 1)
                act.wait_ge(m_win, g * FC + FC)
                x_high(g * 2 + NG + 1)
                shared_expert(g + NG)

            all_groups(act, route_groups)
            tiles(0)
            act.wait_ge(c_up, TILES)
            act.wait_ge(c_hid, TILES)
            act.wait_ge(c_down, TILES)
            all_groups(act, mix_groups)
            tiles(1)

        @block.tensor
        def _(pe):
            pe.wait_ge(s_const, CONSTS)
            pe.wait_ge(s_whi, LOADS_A)
            pe.wait_ge(s_wlo, LOADS_A)

            def turn(m, src):
                pe.wait_ge(s_norm, m + 1)
                wait(pe, s_xthi, m)
                wait(pe, s_xtlo, m)
                for k in range(KC):
                    for i in range(G):
                        last = pe.transpose(pT[:, k, i * P:(i + 1) * P], src[:, i, k * P:(k + 1) * P], ident[:])
                last.then_inc(s_xt, 1)

            xt = (xt_hi, xt_lo)

            def cols(pair, at, n):
                return tuple(t[:, at:at + n] for t in pair)

            def project(out_ap, k_operands, group=True):
                products = [ab for s, m in k_operands for ab in split3(s, m)]
                for c, (s, m) in enumerate(products):
                    last = pe.matmul(out_ap, s, m, start=(c == 0), stop=(c == len(products) - 1))
                return last

            def ffn_group(n, m):
                pe.wait_ge(s_xthi, m + 1)
                pe.wait_ge(s_xtlo, m + 1)
                wait(pe, s_ranked, n)
                for i in range(G):
                    last = project(p_gate[:, i, :], [(cols(xt, k * GT + i * P, P), cols(gate, k * E, E))
                                                     for k in range(KC)])
                last.then_inc(s_gate, 1)
                wait(pe, s_hid, n)
                for h in range(2):
                    last = project(pU[:, h, :], [(cols(up_s, k * HU + h * H, H), cols(xt, k * GT, GT))
                                                 for k in range(KC)])
                last.then_inc(s_up, 1)
                pe.wait_ge(s_members, n + 1)
                for i in range(G):
                    for c in range(i + 1):
                        pe.matmul(p_rank[:, i, :], (before if c == 0 else ones)[:],
                                  members[:, i if c == 0 else c - 1, :], start=(c == 0), stop=(c == i))
                for i in range(G):
                    last = pe.matmul(p_total, ones[:], members[:, i, :], start=(i == 0), stop=(i == G - 1))
                last.then_inc(s_rank, 1)
                pe.wait_ge(s_hidhi, n + 1)
                pe.wait_ge(s_hidlo, n + 1)
                wait(pe, s_sum, n)
                for i in range(G):
                    last = project(pO[:, i // 2, (i % 2) * D:(i % 2 + 1) * D],
                                   [(cols((hid_hi, hid_lo), i * P, P), cols(down_s, 0, D))])
                last.then_inc(s_down, 1)

            def route_groups(g, j, b):
                turn(g, norm[b])
                ffn_group(g, g)

            def tiles(f):
                pe.wait_ge(s_xthi, NG * (1 + 2 * f))
                pe.wait_ge(s_xtlo, NG * (1 + 2 * f))
                pe.wait_ge(s_hid, NG * (f + 1))
                pe.wait_ge(s_ranked, NG * (f + 1))
                pe.wait_ge(s_sum, NG * (f + 1))
                pe.wait_ge(s_tabd, 32 * (f + 1))
                pe.wait_ge(s_whi, LOADS_C)
                pe.wait_ge(s_wlo, LOADS_C)

                def expert_of_tile(q, i):
                    return pe.value_load(tab_row[0:1, bass.ds((q * 2 + i // 2) * 4 + i % 2, 1)],
                                         min_val=0, max_val=E - 1)

                def step(u, q, i):
                    done = f * TILES
                    if in_range(u):
                        pe.wait_ge(c_in[i], (f * (TILES // 4) + q + 1) * 16)
                        wait(pe, c_hi, done + u - 1)
                        wait(pe, c_lo, done + u - 1)
                        for k in range(KC):
                            last = pe.transpose(pT[:, i % 2, k * P:(k + 1) * P], tile_in[i][:, k * P:(k + 1) * P],
                                                ident[:])
                        last.then_inc(c_xt, 1)
                    t = u - 1
                    if in_range(t):
                        i1 = (i - 1) % 4
                        e = expert_of_tile(q if i >= 1 else q - 1, i1)
                        pe.wait_ge(c_hi, done + t + 1)
                        pe.wait_ge(c_lo, done + t + 1)
                        wait(pe, c_hid, done + t - 1)
                        last = project(pU[:, i1 % 2, 0:HU],
                                       [(cols((tile_hi[i1 % 2], tile_lo[i1 % 2]), k * P, P),
                                         tuple(w[:, bass.ds(e * (KC * HU) + k * HU, HU)] for w in up_e))
                                        for k in range(KC)])
                        last.then_inc(c_up, 1)
                    t = u - 2
                    if in_range(t):
                        pe.wait_ge(c_hid, done + t + 1)
                        wait(pe, c_hidhi, done + t - 1)
                        wait(pe, c_hidlo, done + t - 1)
                        pe.transpose(pV[:, i % 2, 0:P], tile_hid[i % 2], ident[:]).then_inc(c_ht, 1)
                    t = u - 3
                    if in_range(t):
                        i3 = (i - 3) % 4
                        e = expert_of_tile(q if i >= 3 else q - 1, i3)
                        pe.wait_ge(c_hidhi, done + t + 1)
                        pe.wait_ge(c_hidlo, done + t + 1)
                        wait(pe, c_out, done + t - 1)
                        last = project(pO[:, i3 % 2, 0:D],
                                       [((tile_hid_hi[i3 % 2], tile_hid_lo[i3 % 2]),
                                         tuple(w[:, bass.ds(e * D, D)] for w in down_e))])
                        last.then_inc(c_down, 1)

                all_tiles(pe, step)

            def mix_groups(g, j, b):
                turn(g * 2 + NG, norm[0])

                def w_in_chunk(f):
                    w = (pU, pV)[f % 2]
                    if f == 0:
                        pe.wait_ge(s_xthi, g * 2 + NG + 1)
                        pe.wait_ge(s_xtlo, g * 2 + NG + 1)
                        pe.wait_ge(s_hid, g + NG)
                    elif f == 1:
                        pe.wait_ge(s_ranked, g + NG)
                    else:
                        pe.wait_ge(m_xc, g * FC + f - 1)
                        pe.wait_ge(m_sz, g * FC + f - 1)
                    for h in range(2):
                        last = project(w[:, h, :], [(cols(win, k * 2 * M + h * M + f * P, P), cols(xt, k * GT, GT))
                                                    for k in range(KC)])
                    last.then_inc(m_win, 1)

                def w_out_chunk(f):
                    if f == 0:
                        pe.wait_ge(s_sum, g + NG)
                    pe.wait_ge(m_mixhi, g * FC + f + 1)
                    pe.wait_ge(m_mixlo, g * FC + f + 1)
                    mix = (mix_hi[f % 2], mix_lo[f % 2])
                    for i in range(G):
                        for c, (s, m) in enumerate(split3(cols(mix, i * P, P), cols(wout, f * D, D))):
                            last = pe.matmul(pO[:, i // 2, (i % 2) * D:(i % 2 + 1) * D], s, m,
                                             start=(f == 0 and c == 0 and i % 2 == 0),
                                             stop=(f == FC - 1 and c == 2), skip_group_check=True)
                    last.then_inc(m_wout, 1)

                for f in range(FC):
                    w_in_chunk(f)
                    if f >= 2:
                        w_out_chunk(f - 2)
                w_out_chunk(FC - 2)
                w_out_chunk(FC - 1)
                turn(g * 2 + NG + 1, norm[1])
                pe.wait_ge(m_xc, g * FC + FC)
                pe.wait_ge(m_sz, g * FC + FC)
                pe.wait_ge(m_x3, g + 1)
                ffn_group(g + NG, g * 2 + NG + 1)

            all_groups(pe, route_groups)
            tiles(0)
            pe.wait_ge(s_whi, len(loads))
            pe.wait_ge(s_wlo, len(loads))
            pe.wait_ge(c_out, TILES)
            all_groups(pe, mix_groups)
            tiles(1)

        @block.vector
        def _(dve):
            dve.memset(counts[:], 0.0).then_inc(s_zero, 1)
            for i, (pair, at, cols, scale, _) in enumerate(loads):
                dve.wait_ge(s_whi, i + 1)
                dve.scalar_tensor_tensor(pair[1][:, at:at + cols], stage[i % 2][:, 0:cols], scale,
                                         pair[0][:, at:at + cols], ALU.mult, ALU.subtract).then_inc(s_wlo, 1)
            dve.wait_ge(s_zero, 1)
            dve.wait_ge(s_small, 48)
            dve.wait_ge(s_const, CONSTS)

            def normalise(m, src, dst, free):
                for i in range(G):
                    last = dve.bn_stats(stats[:, i, :], src[:, i, :])
                last.then_inc(s_stats, 1)
                dve.wait_ge(s_stats, m + 1)
                dve.sem_inc(s_passed_dve, 1)
                for i in range(G):
                    last = dve.bn_aggr(mean_var[:, i, :], stats[:, i, :])
                last.then_inc(s_aggr, 1)
                dve.wait_ge(s_aggr, m + 1)
                wait(dve, s_rstd, m)
                dve.tensor_scalar(var_eps[:], mean_var[:, :, 1], EPS, None, ALU.add).then_inc(s_vareps, 1)
                free()
                dve.wait_ge(s_rstd, m + 1)
                for i in range(G):
                    last = dve.tensor_scalar(dst[:, i, :], src[:, i, :], mean_var[:, i, 0:1], rstd[:, i:i + 1],
                                             ALU.subtract, ALU.mult)
                last.then_inc(s_norm, 1)

            def x_low(m):
                dve.wait_ge(s_xthi, m + 1)
                for k in range(KC):
                    last = dve.tensor_tensor(xt_lo[:, k * GT:(k + 1) * GT], pT[:, k, :],
                                             xt_hi[:, k * GT:(k + 1) * GT], ALU.subtract)
                last.then_inc(s_xtlo, 1)

            def per_choice(ap):
                return ap.unsqueeze(2).to_broadcast([P, G, K, E])

            def route(f, n, b):
                k = [0]
                g = n - f * NG

                def then(ins):
                    k[0] += 1
                    ins.then_inc(s_route, 1)
                    dve.wait_ge(s_route, n * ROUTE_STEPS + k[0])

                dve.wait_ge(s_gate, n + 1)
                then(dve.tensor_tensor(logit[:], p_gate, gate_bias[:].unsqueeze(1).to_broadcast([P, G, E]), ALU.add))
                then(dve.tensor_scalar(logit[:], logit[:], SATURATED, None, ALU.min))
                dve.sem_inc(s_passed_dve, 1)
                for i in range(G):
                    last = dve.max(best[:, i, :], logit[:, i, :])
                then(last)
                dve.sem_inc(s_passed_dve, 1)
                for i in range(G):
                    last = dve.max_index(best_at[:, i, :], best[:, i, :], logit[:, i, :])
                then(last)
                dve.tensor_copy(logit_of[:, bass.ds(g * G * K, G * K)].rearrange("p (i k) -> p i k", k=K),
                                best[:, :, 0:K])
                then(dve.tensor_copy(chosen[:].rearrange("p (i k) -> p i k", k=K), best_at[:, :, 0:K]))
                dve.tensor_copy(expert_of[:, bass.ds(g * G * K, G * K)], chosen[:])
                then(dve.tensor_tensor(onehot[:], chosen[:].unsqueeze(2).to_broadcast([P, G * K, E]),
                                       expert_ids[:].unsqueeze(1).to_broadcast([P, G * K, E]), ALU.is_equal))
                wait(dve, s_rank, n)
                dve.tensor_tensor(members[:], onehot[:, 0::K, :], onehot[:, 1::K, :], ALU.add).then_inc(s_members, 1)
                dve.wait_ge(s_rank, n + 1)
                then(dve.tensor_tensor(rank_all[:], p_rank, counts[:, f, :].unsqueeze(1).to_broadcast([P, G, E]),
                                       ALU.add))
                dve.tensor_tensor(counts[:, f, :], counts[:, f, :], p_total, ALU.add).then_inc(s_ranked, 1)
                dve.wait_ge(s_ranked, n + 1)
                then(dve.tensor_tensor(rank_pick[:].rearrange("p (i k) e -> p i k e", k=K),
                                       onehot[:].rearrange("p (i k) e -> p i k e", k=K),
                                       per_choice(rank_all[:]), ALU.mult))
                then(dve.tensor_reduce(rank[:], rank_pick[:], AX.X, ALU.add))
                dve.tensor_copy(rank_of[:, bass.ds(g * G * K, G * K)], rank[:])
                then(dve.tensor_copy(rank_i[:], rank[:]))
                dve.tensor_scalar(slot_row[:], rank_i[:], P - 1, (E * COLS).bit_length() - 1,
                                  ALU.bitwise_and, ALU.logical_shift_left)
                then(dve.tensor_scalar(slot_col[:], rank_i[:], P.bit_length() - 1, None, ALU.logical_shift_right))
                then(dve.scalar_tensor_tensor(slot_ec[:], chosen[:], float(COLS), slot_col[:], ALU.mult, ALU.add))
                j_done = SCAT * (g_pair[0] + f * NP)
                wait(dve, s_scat[b], j_done)
                dve.tensor_tensor(slot[b][:], slot_ec[:], slot_row[:], ALU.add).then_inc(s_slot, 1)
                assert k[0] == ROUTE_STEPS

            g_pair = [0]
            ROUTE_STEPS = 12

            def ffn_group(f, n, m, j, b):
                x_low(m)
                g_pair[0] = j
                route(f, n, b)
                dve.wait_ge(s_silu, n + 1)
                wait(dve, s_hidhi, n)
                dve.tensor_tensor(hid[:], silu_g[:], pU[:, 1, :], ALU.mult).then_inc(s_hid, 1)
                dve.wait_ge(s_hidhi, n + 1)
                wait(dve, s_down, n)
                dve.tensor_tensor(hid_lo[:], hid[:], hid_hi[:], ALU.subtract).then_inc(s_hidlo, 1)
                dve.wait_ge(s_down, n + 1)
                dve.wait_ge(s_base, n + 1)
                for h in range(2):
                    half = base[b][:, 2 * h:2 * h + 2, :].rearrange("p i d -> p (i d)")
                    last = dve.tensor_tensor(half, pO[:, h, :], half, ALU.add)
                last.then_inc(s_sum, 1)

            def route_groups(g, j, b):
                dve.wait_ge(s_rows[b], (j + 1) * 16)

                def free():
                    wait(dve, s_xt, g - 1)
                    wait(dve, s_half, g - 1)
                    wait(dve, s_normed[b], j * 16)

                normalise(g, rows[b], norm[b], free)
                wait(dve, s_up, g)
                ffn_group(0, g, g, j, b)

            def plan(f):
                k = [0]

                def then(ins):
                    k[0] += 1
                    ins.then_inc(s_plan, 1)
                    dve.wait_ge(s_plan, f * PLAN_STEPS + k[0])

                then(dve.tensor_scalar(tiles_i[:], counts[:, f, :], float(P - 1), None, ALU.add))
                then(dve.tensor_scalar(tiles_i[:], tiles_i[:], P.bit_length() - 1, None, ALU.logical_shift_right))
                then(dve.tensor_copy(tiles_f[:], tiles_i[:]))
                then(dve.tensor_tensor_scan(tiles_upto[:], ones_e[:], tiles_f[:], 0.0, ALU.mult, ALU.add))
                then(dve.tensor_tensor(passed[:], tile_ids[:].unsqueeze(2).to_broadcast([P, 2, E]),
                                       tiles_upto[:].unsqueeze(1).to_broadcast([P, 2, E]), ALU.is_ge))
                then(dve.tensor_tensor(passed_n[:], passed[:], tiles_f[:].unsqueeze(1).to_broadcast([P, 2, E]),
                                       ALU.mult))
                dve.tensor_reduce(tab_e[:], passed[:], AX.X, ALU.add)
                then(dve.tensor_reduce(tab_s[:], passed_n[:], AX.X, ALU.add))
                then(dve.tensor_scalar(tab_e[:], tab_e[:], float(E - 1), None, ALU.min))
                then(dve.tensor_tensor(tab_s[:], tile_ids[:], tab_s[:], ALU.subtract))
                then(dve.scalar_tensor_tensor(tab_s[:], tab_e[:], float(COLS), tab_s[:], ALU.mult, ALU.add))
                if f == 1:
                    dve.wait_ge(s_tabd, 32)
                dve.tensor_copy(tab_i[:, 0, :], tab_e[:])
                dve.tensor_scalar(tab_i[:, 1, :], tab_s[:], float(E * COLS - 1), None, ALU.min).then_inc(s_tab, 1)
                then(dve.tensor_tensor(first_row[:], tiles_upto[:], tiles_f[:], ALU.subtract))
                then(dve.tensor_scalar(first_row[:], first_row[:], float(P), None, ALU.mult))
                wide = rows[0][:].rearrange("p i (c e) -> p (i c) e", e=E)
                half = NT * K // 2
                dve.wait_ge(s_sum, NG * (f + 1))
                for h in range(2):
                    part = slice(h * half, (h + 1) * half)
                    then(dve.tensor_tensor(wide, expert_of[:, part].unsqueeze(2).to_broadcast([P, half, E]),
                                           expert_ids[:].unsqueeze(1).to_broadcast([P, half, E]), ALU.is_equal))
                    then(dve.tensor_tensor(wide, wide, first_row[:].unsqueeze(1).to_broadcast([P, half, E]),
                                           ALU.mult))
                    then(dve.tensor_reduce(expert_of[:, part], wide, AX.X, ALU.add))
                then(dve.tensor_tensor(position[:], expert_of[:], rank_of[:], ALU.add))
                dve.wait_ge(s_exp, f + 1)
                then(dve.tensor_scalar(exp_neg, exp_neg, 1.0, None, ALU.add))
                then(dve.tensor_tensor(denom[:], exp_neg[:, :, 0], exp_neg[:, :, 1], ALU.add))
                then(dve.reciprocal(denom[:], denom[:]))
                dve.tensor_tensor(weight[:, :, 0], exp_neg[:, :, 1], denom[:], ALU.mult)
                dve.tensor_tensor(weight[:, :, 1], exp_neg[:, :, 0], denom[:], ALU.mult).then_inc(s_pos, 1)
                assert k[0] == PLAN_STEPS

            PLAN_STEPS = 22

            def tiles(f):
                dve.wait_ge(s_up, NG * (f + 1))
                dve.wait_ge(s_down, NG * (f + 1))

                def step(u, q, i):
                    done = f * TILES
                    if in_range(u):
                        dve.wait_ge(c_hi, done + u + 1)
                        wait(dve, c_up, done + u - 1)
                        dve.tensor_tensor(tile_lo[i % 2], pT[:, i % 2, 0:D], tile_hi[i % 2], ALU.subtract)\
                           .then_inc(c_lo, 1)
                    t = u - 1
                    if in_range(t):
                        c = (i - 1) % 2
                        dve.wait_ge(c_silu, done + t + 1)
                        wait(dve, c_ht, done + t - 1)
                        dve.tensor_tensor(tile_hid[c], tile_silu[c], pU[:, c, H:HU], ALU.mult).then_inc(c_hid, 1)
                    t = u - 2
                    if in_range(t):
                        dve.wait_ge(c_hidhi, done + t + 1)
                        wait(dve, c_down, done + t - 1)
                        dve.tensor_tensor(tile_hid_lo[i % 2], pV[:, i % 2, 0:P], tile_hid_hi[i % 2], ALU.subtract)\
                           .then_inc(c_hidlo, 1)

                all_tiles(dve, step)

            def combine(f, g, j, b):
                n = g + f * NG
                wait(dve, m_comb, n)
                dve.tensor_copy(weight_now[:].rearrange("p (i k) -> p i k", k=K), weight[:, bass.ds(g * G, G), :])\
                   .then_inc(m_add, 1)
                dve.wait_ge(s_rows[b], (j + (f + 1) * NP + 1) * 16)
                dve.wait_ge(m_picked, (n + 1) * SCAT)
                for k in range(K):
                    dve.wait_ge(m_add, n * 2 + 1 + k)
                    for i in range(G):
                        last = dve.scalar_tensor_tensor(rows[b][:, i, :], picked[:, i, k, :],
                                                        weight_now[:, i * K + k:i * K + k + 1], rows[b][:, i, :],
                                                        ALU.mult, ALU.add)
                    last.then_inc(m_add if k == 0 else m_comb, 1)

            def mix_groups(g, j, b):
                combine(0, g, j, b)
                dve.wait_ge(m_comb, g + 1)

                def norm0_free():
                    dve.wait_ge(s_xt, g * 2 + NG - 1)

                normalise(g * 2 + NG, rows[b], norm[0], norm0_free)
                dve.wait_ge(s_up, g + NG)
                x_low(g * 2 + NG)
                for f in range(FC):
                    c = g * FC + f
                    i = f % 2
                    if b == 0:
                        dve.memset(xc[i][:, 0:TAPS - 1], 0.0).then_inc(m_halo, 1)
                        dve.wait_ge(m_xc, c + 1)
                        dve.tensor_copy(halo[:, f, :], xc[i][:, GT:GT + TAPS - 1]).then_inc(m_halo, 1)
                    else:
                        dve.tensor_copy(xc[i][:, 0:TAPS - 1], halo[:, f, :]).then_inc(m_halo, 2)
                        dve.wait_ge(m_xc, c + 1)
                    dve.wait_ge(m_halo, (c + 1) * 2)
                    wait(dve, m_mixhi, c - 1)
                    wait(dve, m_mixlo, c - 1)
                    dve.tensor_scalar(conv[i][:], xc[i][:, TAPS - 1:], taps[:, f, TAPS - 1:TAPS],
                                      conv_bias[:, f:f + 1], ALU.mult, ALU.add).then_inc(m_tap, 1)
                    for k in range(TAPS - 1):
                        dve.wait_ge(m_tap, c * TAPS + k + 1)
                        dve.scalar_tensor_tensor(conv[i][:], xc[i][:, k:k + GT], taps[:, f, k:k + 1], conv[i][:],
                                                 ALU.mult, ALU.add).then_inc(m_tap, 1)
                    dve.wait_ge(m_xa, c + 1)
                    dve.wait_ge(m_sz, c + 1)
                    dve.tensor_tensor(conv[i][:], conv[i][:], silu_z[i][:], ALU.mult).then_inc(m_mix, 1)
                    dve.wait_ge(m_mixhi, c + 1)
                    wait(dve, m_wout, c - 1)
                    dve.tensor_tensor(mix_lo[i][:], conv[i][:], mix_hi[i][:], ALU.subtract).then_inc(m_mixlo, 1)
                dve.wait_ge(m_wout, g * FC + FC)
                for h in range(2):
                    half = rows[b][:, 2 * h:2 * h + 2, :].rearrange("p i d -> p (i d)")
                    last = dve.tensor_tensor(half, pO[:, h, :], half, ALU.add)
                last.then_inc(m_x3, 1)
                dve.wait_ge(m_x3, g + 1)

                def norm1_free():
                    dve.wait_ge(s_xt, g * 2 + NG)
                    dve.wait_ge(s_half, g + NG)
                    dve.wait_ge(s_normed[1 - b], (j + NP + b) * 16)

                normalise(g * 2 + NG + 1, rows[b], norm[1], norm1_free)
                ffn_group(1, g + NG, g * 2 + NG + 1, j, b)

            all_groups(dve, route_groups)
            dve.sem_inc(s_logits, 1)
            plan(0)
            tiles(0)
            dve.wait_ge(c_xt, TILES)
            all_groups(dve, mix_groups)
            dve.sem_inc(s_logits, 1)
            plan(1)
            tiles(1)

            def output_groups(g, j, b):
                combine(1, g, j, b)

            all_groups(dve, output_groups)


_INS = ["x", "w_in", "w_conv", "b_conv", "w_out"]
_FFN = ["gate_w", "gate_b", "shared_wg", "shared_wu", "shared_wd", "experts_wg", "experts_wu", "experts_wd"]


def kernel(**inputs):
    import numpy as np
    import concourse.bacc as bacc
    from concourse.bass_utils import run_bass_kernel_spmd

    nc = bacc.Bacc("TRN2", target_bir_lowering=False, num_devices=1)
    arrays, args = {}, []
    for name in [f"L0_attn_{n}" for n in _INS] + [f"L0_ffn_{n}" for n in _FFN]:
        a = np.ascontiguousarray(inputs[name])
        arrays[f"in_{name}"] = a
        args.append(nc.dram_tensor(f"in_{name}", a.shape, mybir.dt.from_np(a.dtype), kind="ExternalInput").ap())
    shape = inputs["L0_attn_x"].shape
    args.append(nc.dram_tensor("out_0", shape, F32, kind="ExternalOutput").ap())
    build_macaron(nc, *args)
    r = run_bass_kernel_spmd(nc, [arrays], core_ids=[0])
    return r.results[0]["out_0"]
```

```python
from contextlib import ExitStack

import concourse.bass as bass
from concourse import mybir
from concourse.alu_op_type import AluOpType as ALU

ACT = mybir.ActivationFunctionType
AX = mybir.AxisListType
F32 = mybir.dt.float32
F32R = mybir.dt.float32r
BF16 = mybir.dt.bfloat16
I32 = mybir.dt.int32
U32 = mybir.dt.uint32

P = 128
G = 4
GT = G * P
EPS = 1e-5
SATURATED = 17.33


def wait(engine, semaphore, value):
    if not (isinstance(value, int) and value <= 0):
        engine.wait_ge(semaphore, value)


def build_macaron(nc, x, w_in, w_conv, b_conv, w_out, gate_w, gate_b, shared_wg, shared_wu, shared_wd,
                  experts_wg, experts_wu, experts_wd, out):
    B, L, D = x.shape
    T = B * L
    E, _, H = experts_wg.shape
    M = w_out.shape[0]
    TAPS = w_conv.shape[2]
    K = 2
    KC = D // P
    FC = M // P
    NT = T // P
    NG = T // GT
    NP = NG // 2
    HU = 2 * H
    RING = 8
    TILES = -(-(T * K // P + E - 1) // RING) * RING
    TAB = 5
    COLS = T // P
    assert D == 256 and H == P and L == 2 * GT and M == FC * P and E == 16 and TILES <= 4 * P

    x_rows = x.rearrange("b l d -> (b l) d")
    out_rows = out.rearrange("b l d -> (b l) d")

    def grouped(rows):
        return rows.rearrange("(i p) d -> p i d", p=P)

    normed = [nc.dram_tensor(f"normed{f}", (T, D), F32).ap() for f in range(2)]
    sums = [nc.dram_tensor(f"sums{f}", (T, D), F32).ap() for f in range(2)]
    expert_out = [nc.dram_tensor(f"expert_out{f}", (TILES * P, D), F32).ap() for f in range(2)]
    lists = [nc.dram_tensor(f"lists{f}", (P * E * COLS, 1), I32).ap() for f in range(2)]
    tables = [nc.dram_tensor(f"tables{f}", (P, TAB), I32).ap() for f in range(2)]

    with ExitStack() as ctx:
        def sb(name, shape, dt=F32):
            return ctx.enter_context(nc.sbuf_tensor(name, shape, dt))

        def sem(name):
            return ctx.enter_context(nc.semaphore(name))

        def parts(name, shape):
            return sb(name + "_hi", shape, F32R), sb(name + "_lo", shape, F32R)

        gate = parts("gate", [P, KC * E])
        up_s = parts("up_s", [P, KC * HU])
        up_e = parts("up_e", [P, E * KC * HU])
        down_e = parts("down_e", [P, E * D])
        win = parts("win", [P, KC * 2 * M])
        down_s = sb("down_s", [P, D])
        wout = sb("wout", [P, FC * D])
        taps = sb("taps", [P, FC, TAPS])
        conv_bias = sb("conv_bias", [P, FC])
        gate_bias = sb("gate_bias", [P, E])

        ident = sb("ident", [P, P])
        before = sb("before", [P, P], BF16)
        ones = sb("ones", [P, P], BF16)
        expert_ids = sb("expert_ids", [P, E])
        tile_ids = sb("tile_ids", [P, 4])
        ones_e = sb("ones_e", [P, E])
        minus_half = sb("minus_half", [P, G])
        token_ids = sb("token_ids", [P, NT], I32)

        rows = [sb(f"rows{b}", [P, G, D]) for b in range(2)]
        norm = [sb(f"norm{b}", [P, G, D]) for b in range(2)]
        base = [sb(f"base{b}", [P, G, D]) for b in range(2)]
        xt = [parts(f"xt{i}", [P, KC * GT]) for i in range(2)]
        silu_g = sb("silu_g", [P, GT])
        hid = sb("hid", [P, GT])
        picked = sb("picked", [P, G, K, D])
        xc = [sb(f"xc{i}", [P, GT + TAPS - 1]) for i in range(2)]
        halo = sb("halo", [P, FC, TAPS - 1])
        silu_z = [sb(f"silu_z{i}", [P, GT]) for i in range(2)]
        conv = [sb(f"conv{f}", [P, GT]) for f in range(FC)]
        hid_parts = parts("hid_parts", [P, 2 * P])

        stats = sb("stats", [P, G, 6])
        mean_var = sb("mean_var", [P, G, 2])
        var_eps = sb("var_eps", [P, G])
        rstd = sb("rstd", [P, G])
        base_scale = sb("base_scale", [P, G])
        base_shift = sb("base_shift", [P, G])
        logit = sb("logit", [P, G, E])
        best = sb("best", [P, G, 8])
        best_at = sb("best_at", [P, G, 8], U32)
        chosen = sb("chosen", [P, G * K])
        onehot = sb("onehot", [P, G * K, E])
        members = sb("members", [P, G, E], BF16)
        rank_all = sb("rank_all", [P, G, E])
        rank_pick = sb("rank_pick", [P, G * K, E])
        rank = sb("rank", [P, G * K])
        rank_i = sb("rank_i", [P, G * K], I32)
        slot_row = sb("slot_row", [P, G * K], I32)
        slot_col = sb("slot_col", [P, G * K], I32)
        slot_ec = sb("slot_ec", [P, G * K])
        slot = [sb(f"slot{b}", [P, G * K], U32) for b in range(2)]
        token = [sb(f"token{b}", [P, G], I32) for b in range(2)]
        counts = sb("counts", [P, 2, E])
        expert_of = sb("expert_of", [P, NT * K])
        rank_of = sb("rank_of", [P, NT * K])
        logit_of = sb("logit_of", [P, NT * K])
        position = sb("position", [P, NT * K], I32)
        weight = sb("weight", [P, NT, K])
        exp_neg = logit_of[:].rearrange("p (t k) -> p t k", k=K)
        denom = sb("denom", [P, NT])
        tiles_i = sb("tiles_i", [P, E], I32)
        tiles_f = sb("tiles_f", [P, E])
        tiles_upto = sb("tiles_upto", [P, E])
        first_row = sb("first_row", [P, E])
        passed = sb("passed", [P, 4, E])
        passed_n = sb("passed_n", [P, 4, E])
        tab_e = sb("tab_e", [P, 4])
        tab_s = sb("tab_s", [P, 4])
        tab_pack = sb("tab_pack", [P, 4])
        tab_i = sb("tab_i", [P, TAB], I32)
        tab_row = sb("tab_row", [1, TAB * TILES // 4], I32)
        clear = sb("clear", [P, E * COLS], I32)
        gather_at = sb("gather_at", [P, RING], U32)
        weight_now = sb("weight_now", [P, G * K])
        pick_at = [sb(f"pick_at{b}", [P, G * K], U32) for b in range(2)]

        pT = ctx.enter_context(nc.psum_tensor("pT", [P, 2, 512], F32))
        pR = ctx.enter_context(nc.psum_tensor("pR", [P, 4, 512], F32))
        pO = ctx.enter_context(nc.psum_tensor("pO", [P, 2, 512], F32))
        p_gate = pR[:, 2, 0:G * E].rearrange("p (i e) -> p i e", i=G)
        p_up = (pR[:, 3, :], pR[:, 0, :])
        p_rank = pR[:, 3, 0:G * E].rearrange("p (i e) -> p i e", i=G)
        p_total = pR[:, 3, G * E:G * E + E]
        p_mix = [(pR[:, (f % 2) * 2, :], pR[:, (f % 2) * 2 + 1, :]) for f in range(FC - 1)]
        p_mix.append((pR[:, 1, :], pR[:, 2, :]))

        tile_in = [norm[i // 4][:, i % 4, :] for i in range(RING)]
        tile_x = [tuple(t[:, c * D:(c + 1) * D] for t in xt[0]) for c in range(2)]
        tile_silu = [silu_g[:, c * H:(c + 1) * H] for c in range(2)]
        tile_hid = [hid[:, c * H:(c + 1) * H] for c in range(2)]
        tile_hidp = [tuple(t[:, c * P:(c + 1) * P] for t in hid_parts) for c in range(2)]
        tile_out = [base[i // 4][:, i % 4, :] for i in range(RING)]
        p_tile_up = [pR[:, c, 0:HU] for c in range(2)]
        p_tile_ht = [pR[:, 2 + c, 0:P] for c in range(2)]
        picked_in = [[[picked[:, i, k, :] for k in range(K)] for i in range(G)],
                     [[norm[i // 2][:, (i % 2) * K + k, :] for k in range(K)] for i in range(G)]]

        stage = [picked[:, 2 * i:2 * i + 2, :, :].rearrange("p i k d -> p (i k d)") for i in range(2)]
        loads = []

        def piece(pair, at, cols, scale, *sources):
            loads.append((pair, at, cols, scale, sources))

        piece(gate, 0, KC * E, 1.0, (0, E, E, gate_w.rearrange("(k p) e -> p k e", p=P)))
        piece(up_s, 0, KC * HU, 1.0, (0, H, HU, shared_wg.rearrange("(k p) h -> p k h", p=P)),
              (H, H, HU, shared_wu.rearrange("(k p) h -> p k h", p=P)))
        LOADS_A = len(loads)
        win_view = w_in.rearrange("(k p) m -> p k m", p=P)
        for k in range(KC):
            piece(win, k * 2 * M, 2 * M, 1.0, (0, 2 * M, 2 * M, win_view[:, k:k + 1, :]))
        g_view = experts_wg.rearrange("e (k p) h -> p (e k) h", p=P)
        u_view = experts_wu.rearrange("e (k p) h -> p (e k) h", p=P)
        d_view = experts_wd.rearrange("e h d -> h e d")
        UP2, DOWN2 = 2 * KC * HU, 2 * D
        assert E == 2 * NP
        loaded = {0: 0, 1: 0}
        load_ready = []
        for i, (_, _, _, _, sources) in enumerate(loads):
            loaded[i % 2] += 16 * len(sources)
            load_ready.append(loaded[i % 2])

        s_const = sem("s_const")
        s_zero = sem("s_zero")
        s_small = sem("s_small")
        s_whole = sem("s_whole")
        s_half_w = sem("s_half_w")
        s_cleared = sem("s_cleared")
        s_stage = [sem("s_stage0"), sem("s_stage1")]
        s_whi = sem("s_whi")
        s_wlo = sem("s_wlo")
        s_passed_pool = sem("s_passed_pool")
        s_passed_dve = sem("s_passed_dve")
        s_passed_sp = sem("s_passed_sp")
        s_rows = [sem("s_rows0"), sem("s_rows1")]
        s_stats = sem("s_stats")
        s_aggr = sem("s_aggr")
        s_vareps = sem("s_vareps")
        s_rstd = sem("s_rstd")
        s_shift = sem("s_shift")
        s_norm = sem("s_norm")
        s_base = sem("s_base")
        s_xt = sem("s_xt")
        s_xthi = sem("s_xthi")
        s_xtlo = sem("s_xtlo")
        s_gate = sem("s_gate")
        s_logit = sem("s_logit")
        s_up = sem("s_up")
        s_silu = sem("s_silu")
        s_hid = sem("s_hid")
        s_down = sem("s_down")
        s_sum = sem("s_sum")
        s_route = sem("s_route")
        s_members = sem("s_members")
        s_rank = sem("s_rank")
        s_ranked = sem("s_ranked")
        s_slot = sem("s_slot")
        s_token = sem("s_token")
        s_scat = [sem("s_scat0"), sem("s_scat1")]
        s_normed = [sem("s_normed0"), sem("s_normed1")]
        s_sums = [sem("s_sums0"), sem("s_sums1")]
        s_plan = sem("s_plan")
        s_tab = sem("s_tab")
        s_tabd = sem("s_tabd")
        s_exp = sem("s_exp")
        s_pos = sem("s_pos")
        c_at = [sem(f"c_at{i}") for i in range(RING)]
        c_in = [sem(f"c_in{i}") for i in range(RING)]
        c_xt = sem("c_xt")
        c_hi = sem("c_hi")
        c_lo = sem("c_lo")
        c_up = sem("c_up")
        c_silu = sem("c_silu")
        c_hid = sem("c_hid")
        c_ht = sem("c_ht")
        c_hidhi = sem("c_hidhi")
        c_hidlo = sem("c_hidlo")
        c_down = sem("c_down")
        c_out = sem("c_out")
        c_stored = [sem(f"c_stored{i}") for i in range(RING)]
        m_at = sem("m_at")
        m_picked = [sem("m_picked0"), sem("m_picked1")]
        m_weight = sem("m_weight")
        m_add = sem("m_add")
        m_comb = sem("m_comb")
        m_win = sem("m_win")
        m_xc = sem("m_xc")
        m_tap0 = sem("m_tap0")
        m_sz = sem("m_sz")
        m_halo = sem("m_halo")
        m_tap = sem("m_tap")
        m_xa = sem("m_xa")
        m_mix = sem("m_mix")
        m_wout = sem("m_wout")
        m_x3 = sem("m_x3")
        s_out = [sem("s_out0"), sem("s_out1")]

        CONSTS = 11
        SCAT = 16 * G * K
        NQ = TILES // RING
        UP_LAG, HT_LAG, DOWN_LAG = 1, 2, 3
        WEIGHTS = len(loads) + 2 * NP
        T3 = TAPS - 1
        block = ctx.enter_context(nc.Block())

        def split3(a, b):
            return [(a[0], b[0]), (a[0], b[1]), (a[1], b[0])]

        def mixer_norm(g):
            return NG if isinstance(g, int) and g == 0 else g * 2 + NG - 1

        def ffn_norm(g):
            return 3 * NG - 1 if isinstance(g, int) and g == NG - 1 else g * 2 + NG + 2

        def all_groups(engine, body):
            for b in range(2):
                body(b, 0, b)
            with engine.Fori(1, NP - 1) as j:
                for b in range(2):
                    body(j * 2 + b, j, b)
            for b in range(2):
                body(NG - 2 + b, NP - 1, b)

        def neighbours(g, j, b):
            before_g = None if isinstance(g, int) and g == 0 else (g - 1, j if b else j - 1, 1 - b)
            after_g = None if isinstance(g, int) and g >= NG - 1 else (g + 1, j + 1 if b else j, 1 - b)
            return before_g, after_g

        def all_tiles(engine, body, steps):
            for i in range(RING):
                body(i, 0, i)
            with engine.Fori(1, NQ) as q:
                for i in range(RING):
                    body(q * RING + i, q, i)
            for i in range(steps):
                body(TILES + i, NQ + i // RING, i % RING)

        def back(u, q, i, n):
            t = u - n
            if isinstance(t, int) and not 0 <= t < TILES:
                return None
            return t, q + (i - n) // RING, (i - n) % RING

        @block.sync
        def _(sp):
            def load_rows(src, n, b):
                sp.dma_start(rows[b][:], grouped(src[bass.ds(n * GT, GT), :])).then_inc(s_rows[b], 16)

            def load_piece(i):
                _, _, cols, _, sources = loads[i]
                if i >= 2:
                    sp.wait_ge(s_whi, i - 1)
                    sp.wait_ge(s_wlo, i - 1)
                for at, width, step, src in sources:
                    dst = stage[i % 2][:, 0:cols].rearrange("p (n s) -> p n s", s=step)[:, :, at:at + width]
                    sp.dma_start(dst, src).then_inc(s_stage[i % 2], 16)

            def load_experts(j, b):
                done = j * 2 + b + len(loads) - 1
                sp.wait_ge(s_whi, done)
                sp.wait_ge(s_wlo, done)
                if b == 0:
                    dst = stage[0].rearrange("p (n s) -> p n s", s=HU)
                    for h, view in enumerate((g_view, u_view)):
                        sp.dma_start(dst[:, :, h * H:(h + 1) * H], view[:, bass.ds(j * 2 * KC, 2 * KC), :])\
                            .then_inc(s_stage[0], 16)
                else:
                    sp.dma_start(stage[1][:, 0:DOWN2].rearrange("p (n d) -> p n d", d=D),
                                 d_view[:, bass.ds(j * 2, 2), :]).then_inc(s_stage[1], 16)

            def store_normed(f, g, b):
                sp.wait_ge(s_norm, (g if f == 0 else ffn_norm(g)) + 1)
                sp.dma_start(grouped(normed[f][bass.ds(g * GT, GT), :]), norm[b if f == 0 else 1][:])\
                    .then_inc(s_normed[b], 16)

            def store_sums(f, g, b):
                sp.wait_ge(s_sum, g + f * NG + 1)
                sp.dma_start(grouped(sums[f][bass.ds(g * GT, GT), :]), base[b][:]).then_inc(s_sums[b], 16)

            def groups(f, src):
                def body(g, j, b):
                    before_g, _ = neighbours(g, j, b)
                    store_normed(f, g, b)
                    sp.wait_ge(s_base, g + f * NG + 1)
                    last_pair = isinstance(g, int) and g >= NG - 2
                    if not last_pair:
                        load_rows(src, g + 2, b)
                    if before_g:
                        store_sums(f, before_g[0], before_g[2])
                    if f == 0 and not last_pair:
                        load_experts(j + 1, b)

                all_groups(sp, body)
                store_sums(f, NG - 1, 1)

            def tiles(f):
                sp.wait_ge(s_tab, f + 1)
                sp.dma_start(tables[f], tab_i[:]).then_inc(s_tabd, 16)
                sp.wait_ge(s_tabd, 32 * f + 16)
                sp.dma_start(tab_row[:], tables[f][0:TILES // 4, :].rearrange("(o p) c -> o (p c)", o=1))\
                    .then_inc(s_tabd, 16)
                for b in range(2):
                    sp.wait_ge(s_scat[b], SCAT * NP * (f + 1))
                sp.wait_ge(s_tabd, 32 * (f + 1))
                by_slot = lists[f].rearrange("(p c) o -> p (c o)", p=P)

                def step(u, q, i):
                    if back(u, q, i, 0):
                        col = sp.value_load(tab_row[0:1, bass.ds((q * (RING // 4) + i // 4) * TAB + i % 4, 1)],
                                            min_val=0, max_val=E * COLS - 1)
                        wait(sp, c_in[i], (q + f * NQ) * 16)
                        sp.sem_inc(s_passed_sp, 1)
                        with nc.allow_non_contiguous_dma("128 numbers"):
                            sp.dma_start(gather_at[:, i:i + 1], by_slot[:, bass.ds(col, 1)].bitcast(U32))\
                                .then_inc(c_at[i], 16)

                all_tiles(sp, step, 0)

            load_piece(0)
            load_piece(1)
            for b in range(2):
                load_rows(x_rows, b, b)
            with nc.allow_non_contiguous_dma("small loads"):
                sp.dma_start(gate_bias[:], gate_b.partition_broadcast(P)).then_inc(s_small, 16)
                sp.dma_start(down_s[:], shared_wd).then_inc(s_whole, 16)
                for i in range(2, len(loads)):
                    load_piece(i)
                sp.wait_ge(s_const, CONSTS)
                for f in range(2):
                    sp.dma_start(lists[f].rearrange("(p c) o -> p (c o)", p=P), clear[:]).then_inc(s_cleared, 16)
                sp.dma_start(taps[:], w_conv.rearrange("(f p) o t -> p f (o t)", p=P)).then_inc(s_small, 16)
                sp.dma_start(conv_bias[:], b_conv.rearrange("(f p) -> p f", p=P)).then_inc(s_small, 16)
                sp.dma_start(wout[:].rearrange("p (f d) -> p f d", d=D), w_out.rearrange("(f p) d -> p f d", p=P))\
                    .then_inc(s_small, 16)
            for b in range(2):
                load_experts(0, b)
            groups(0, x_rows)
            tiles(0)
            for b in range(2):
                sp.wait_ge(s_sums[b], 16 * NP)
            for b in range(2):
                load_rows(sums[0], b, b)
            groups(1, sums[0])
            tiles(1)
            for b in range(2):
                sp.wait_ge(s_sums[b], 32 * NP)
            for b in range(2):
                load_rows(sums[1], b, b)

            def store_out(g, j, b):
                sp.wait_ge(m_comb, NG + g + 1)
                sp.dma_start(grouped(out_rows[bass.ds(g * GT, GT), :]), rows[b][:]).then_inc(s_out[b], 16)
                sp.wait_ge(s_out[b], (j + 1) * 16)
                if not (isinstance(g, int) and g >= NG - 2):
                    load_rows(sums[1], g + 2, b)

            all_groups(sp, store_out)
            for b in range(2):
                sp.wait_ge(s_out[b], 16 * NP)

        @block.gpsimd
        def _(pool):
            pool.memset(ident[:], 0.0).then_inc(s_const, 1)
            pool.memset(before[:], 1.0).then_inc(s_const, 1)
            pool.memset(ones[:], 1.0).then_inc(s_const, 1)
            pool.memset(ones_e[:], 1.0).then_inc(s_const, 1)
            pool.memset(minus_half[:], -0.5).then_inc(s_const, 1)
            pool.memset(clear[:], 0).then_inc(s_const, 1)
            pool.iota(expert_ids[:], [[1, E]], base=0, channel_multiplier=0,
                      allow_small_or_imprecise_dtypes=True).then_inc(s_const, 1)
            pool.iota(tile_ids[:], [[1, 4]], base=0, channel_multiplier=4,
                      allow_small_or_imprecise_dtypes=True).then_inc(s_const, 1)
            pool.iota(token_ids[:], [[P, NT]], base=0, channel_multiplier=1).then_inc(s_const, 1)
            pool.wait_ge(s_const, 9)
            pool.affine_select(out=ident[:], in_=ident[:], compare_op=ALU.not_equal, fill=1.0, base=0,
                               pattern=[[-1, P]], channel_multiplier=1).then_inc(s_const, 1)
            pool.affine_select(out=before[:], in_=before[:], compare_op=ALU.is_gt, fill=0.0, base=0,
                               pattern=[[1, P]], channel_multiplier=-1).then_inc(s_const, 1)

            def inverse_std(m):
                pool.wait_ge(s_vareps, m + 1)
                pool.tensor_tensor(rstd[:], var_eps[:], minus_half[:], ALU.pow).then_inc(s_rstd, 1)

            def scatter(f, g, b):
                n = g + f * NG
                pool.wait_ge(s_slot, n + 1)
                pool.tensor_copy(token[b][:], token_ids[:, bass.ds(g * G, G)]).then_inc(s_token, 1)
                pool.wait_ge(s_token, n + 1)
                pool.sem_inc(s_passed_pool, 1)
                for c in range(G * K):
                    pool.indirect_dma_start(lists[f], bass.IndirectOffsetOnAxis(slot[b][:, c:c + 1], 0),
                                            token[b][:, c // K:c // K + 1], None).then_inc(s_scat[b], 16)

            def gather_tiles(f):
                for b in range(2):
                    pool.wait_ge(s_normed[b], 16 * NP * (f + 1))
                pool.wait_ge(s_xt, NG * (1 + 2 * f))

                def gather(t, q, i):
                    wait(pool, c_xt, f * TILES + t - RING + 1)
                    pool.wait_ge(c_at[i], (q + f * NQ + 1) * 16)
                    pool.sem_inc(s_passed_pool, 1)
                    pool.indirect_dma_start(tile_in[i], None, normed[f],
                                            bass.IndirectOffsetOnAxis(gather_at[:, i:i + 1], 0))\
                        .then_inc(c_in[i], 16)

                all_tiles(pool, gather, 0)

            def pick(f, g, b):
                wait(pool, m_comb, g if f == 0 else g + NG - 1)
                pool.tensor_copy(pick_at[b][:], position[:, bass.ds(g * G * K, G * K)]).then_inc(m_at, 1)
                pool.wait_ge(m_at, g + f * NG + 1)
                pool.sem_inc(s_passed_pool, 1)
                for c in range(G * K):
                    pool.indirect_dma_start(picked_in[b * f][c // K][c % K], None, expert_out[f],
                                            bass.IndirectOffsetOnAxis(pick_at[b][:, c:c + 1], 0))\
                        .then_inc(m_picked[b], 16)

            def wait_experts(f):
                pool.wait_ge(s_pos, f + 1)
                pool.wait_ge(c_xt, TILES * (f + 1))
                for i in range(RING):
                    pool.wait_ge(c_stored[i], 16 * NQ * (f + 1))

            def route_groups(g, j, b):
                _, after = neighbours(g, j, b)
                if after:
                    inverse_std(after[0])
                scatter(0, g, b)

            def mix_groups(g, j, b):
                before_g, after = neighbours(g, j, b)
                if before_g:
                    inverse_std(ffn_norm(before_g[0]))
                    if not (isinstance(g, int) and g < 2):
                        scatter(1, g - 2, b)
                if after:
                    inverse_std(mixer_norm(after[0]))
                    if not (isinstance(g, int) and g >= NG - 2):
                        pick(0, g + 2, b)

            inverse_std(0)
            pool.wait_ge(s_cleared, 32)
            all_groups(pool, route_groups)
            gather_tiles(0)
            wait_experts(0)
            pick(0, 0, 0)
            inverse_std(NG)
            pick(0, 1, 1)
            all_groups(pool, mix_groups)
            mix_groups(NG, NP, 0)
            scatter(1, NG - 1, 1)
            gather_tiles(1)
            wait_experts(1)
            all_groups(pool, lambda g, j, b: pick(1, g, b))

        @block.scalar
        def _(act):
            def split_high(i):
                pair, at, cols, scale, _ = loads[i]
                act.wait_ge(s_stage[i % 2], load_ready[i])
                act.activation(pair[0][:, at:at + cols], stage[i % 2][:, 0:cols], ACT.Copy, scale=scale)\
                   .then_inc(s_whi, 1)

            def split_high_experts(j, b):
                act.wait_ge(s_stage[b], (j + 1) * (32, 16)[b] + loaded[b])
                dst, cols, scale = ((up_e, UP2, 1.0), (down_e, DOWN2, 0.5))[b]
                act.activation(dst[0][:, bass.ds(j * cols, cols)], stage[b][:, 0:cols], ACT.Copy, scale=scale)\
                   .then_inc(s_whi, 1)

            def x_high(m, dst):
                act.wait_ge(s_xt, m + 1)
                for k in range(KC):
                    last = act.activation(dst[0][:, k * GT:(k + 1) * GT], pT[:, k, :], ACT.Copy)
                last.then_inc(s_xthi, 1)

            def make_base(f, g, j, b):
                n = g + f * NG
                act.wait_ge(s_shift, n + 1)
                wait(act, s_sums[b], (j + f * NP) * 16)
                if f == 1 and isinstance(g, int) and g < 2:
                    for i in range(RING):
                        act.wait_ge(c_stored[i], 16 * NQ)
                for i in range(G):
                    last = act.activation(base[b][:, i, :], rows[b][:, i, :], ACT.Identity,
                                          bias=base_shift[:, i:i + 1], scale=base_scale[:, i:i + 1])
                last.then_inc(s_base, 1)

            def silu_shared(n):
                act.wait_ge(s_up, n + 1)
                wait(act, s_hid, n)
                act.activation(silu_g[:], p_up[0], ACT.Silu).then_inc(s_silu, 1)

            def route_groups(g, j, b):
                _, after = neighbours(g, j, b)
                silu_shared(g)
                if after:
                    make_base(0, *after)
                split_high_experts(j, b)
                if after:
                    wait(act, s_up, g)
                    x_high(after[0], xt[after[2]])

            def tiles(f):
                act.wait_ge(s_slot, NG * (f + 1))
                act.activation(logit_of[:], logit_of[:], ACT.Exp, scale=-1.0).then_inc(s_exp, 1)
                act.wait_ge(s_up, NG * (f + 1))
                act.wait_ge(s_hid, NG * (f + 1))
                for b in range(2):
                    act.wait_ge(s_sums[b], 16 * NP * (f + 1))

                def step(u, q, i):
                    done = f * TILES
                    if tile := back(u, q, i, 0):
                        t, _, r = tile
                        act.wait_ge(c_xt, t + done + 1)
                        wait(act, c_up, t + done - 1)
                        act.activation(tile_x[r % 2][0], pT[:, r % 2, 0:D], ACT.Copy).then_inc(c_hi, 1)
                    if tile := back(u, q, i, UP_LAG):
                        t, _, r = tile
                        act.wait_ge(c_up, t + done + 1)
                        wait(act, c_hid, t + done - 1)
                        act.activation(tile_silu[r % 2], p_tile_up[r % 2][:, 0:H], ACT.Silu).then_inc(c_silu, 1)
                    if tile := back(u, q, i, HT_LAG):
                        t, _, r = tile
                        act.wait_ge(c_ht, t + done + 1)
                        wait(act, c_down, t + done - 1)
                        act.activation(tile_hidp[r % 2][0], p_tile_ht[r % 2], ACT.Copy).then_inc(c_hidhi, 1)
                    if tile := back(u, q, i, DOWN_LAG):
                        t, round_, r = tile
                        act.wait_ge(c_down, t + done + 1)
                        wait(act, c_stored[r], (round_ + f * NQ) * 16)
                        act.activation(tile_out[r], pO[:, r % 2, 0:D], ACT.Copy).then_inc(c_out, 1)
                    if tile := back(u, q, i, DOWN_LAG + 1):
                        t, _, r = tile
                        act.wait_ge(c_out, t + done + 1)
                        act.dma_start(expert_out[f][bass.ds(t * P, P), :], tile_out[r]).then_inc(c_stored[r], 16)

                all_tiles(act, step, DOWN_LAG + 1)

            def mix_chunk(g, f):
                c = g * FC + f
                act.wait_ge(m_win, c + 1)
                wait(act, m_tap, (c - 1) * T3)
                act.activation(xc[f % 2][:, T3:], p_mix[f][0], ACT.Copy).then_inc(m_xc, 1)
                wait(act, m_wout, c - 3)
                act.activation(conv[f][:], p_mix[f][0], ACT.Identity, bias=conv_bias[:, f:f + 1],
                               scale=taps[:, f, T3:TAPS]).then_inc(m_tap0, 1)
                wait(act, m_mix, c - 1)
                act.activation(silu_z[f % 2][:], p_mix[f][1], ACT.Silu).then_inc(m_sz, 1)

            def silu_conv(g, f):
                c = g * FC + f
                act.wait_ge(m_tap, (c + 1) * T3)
                act.activation(conv[f][:], conv[f][:], ACT.Silu).then_inc(m_xa, 1)

            def mix_groups(g, j, b):
                prev, after = neighbours(g, j, b)
                here = not (isinstance(g, int) and g >= NG)
                if here:
                    mix_chunk(g, 0)
                if prev:
                    make_base(1, *prev)
                if here:
                    mix_chunk(g, 1)
                if prev:
                    wait(act, s_up, prev[0] + NG)
                    x_high(ffn_norm(prev[0]), xt[1])
                if here:
                    silu_conv(g, 0)
                    mix_chunk(g, 2)
                    silu_conv(g, 1)
                if prev:
                    silu_shared(prev[0] + NG)
                if here:
                    mix_chunk(g, 3)
                    silu_conv(g, 2)
                    silu_conv(g, 3)
                if after:
                    act.wait_ge(m_win, (g + 1) * FC)
                    x_high(mixer_norm(after[0]), xt[0])

            split_high(0)
            split_high(1)
            act.wait_ge(s_whole, 16)
            act.activation(down_s[:], down_s[:], ACT.Copy, scale=0.5).then_inc(s_half_w, 1)
            make_base(0, 0, 0, 0)
            x_high(0, xt[0])
            for i in range(2, len(loads)):
                split_high(i)
            act.wait_ge(s_small, 64)
            all_groups(act, route_groups)
            tiles(0)
            act.wait_ge(c_up, TILES)
            act.wait_ge(c_hid, TILES)
            x_high(NG, xt[0])
            all_groups(act, mix_groups)
            mix_groups(NG, NP, 0)
            tiles(1)

        @block.tensor
        def _(pe):
            def turn(m, src, free):
                pe.wait_ge(s_norm, m + 1)
                wait(pe, s_xthi, m)
                wait(pe, s_xtlo, m)
                free()
                for k in range(KC):
                    for i in range(G):
                        last = pe.transpose(pT[:, k, i * P:(i + 1) * P], src[:, i, k * P:(k + 1) * P], ident[:])
                last.then_inc(s_xt, 1)

            def cols(pair, at, n):
                return tuple(t[:, at:at + n] for t in pair)

            def project(out_ap, k_operands):
                products = [ab for s, m in k_operands for ab in split3(s, m)]
                for c, (s, m) in enumerate(products):
                    last = pe.matmul(out_ap, s, m, start=(c == 0), stop=(c == len(products) - 1))
                return last

            def gate_and_up(n, m, x):
                pe.wait_ge(s_xthi, m + 1)
                pe.wait_ge(s_xtlo, m + 1)
                wait(pe, s_logit, n)
                for i in range(G):
                    last = project(p_gate[:, i, :], [(cols(x, k * GT + i * P, P), cols(gate, k * E, E))
                                                     for k in range(KC)])
                last.then_inc(s_gate, 1)
                wait(pe, s_ranked, n)
                wait(pe, s_hid, n)
                for h in range(2):
                    last = project(p_up[h], [(cols(up_s, k * HU + h * H, H), cols(x, k * GT, GT))
                                             for k in range(KC)])
                last.then_inc(s_up, 1)

            def ranks(n):
                pe.wait_ge(s_members, n + 1)
                pe.wait_ge(s_silu, n + 1)
                for i in range(G):
                    for c in range(i + 1):
                        pe.matmul(p_rank[:, i, :], (before if c == 0 else ones)[:],
                                  members[:, i if c == 0 else c - 1, :], start=(c == 0), stop=(c == i))
                for i in range(G):
                    last = pe.matmul(p_total, ones[:], members[:, i, :], start=(i == 0), stop=(i == G - 1))
                last.then_inc(s_rank, 1)

            def down(n, dst):
                pe.wait_ge(s_hid, n + 1)
                for i in range(G):
                    last = pe.matmul(dst[:, i // 2, (i % 2) * D:(i % 2 + 1) * D], hid[:, i * P:(i + 1) * P],
                                     down_s[:], start=True, stop=True)
                last.then_inc(s_down, 1)

            def route_groups(g, j, b):
                _, after = neighbours(g, j, b)
                gate_and_up(g, g, xt[b])
                if after:
                    turn(after[0], norm[after[2]], lambda: None)
                ranks(g)
                wait(pe, s_sum, g)
                down(g, pO)

            def tiles(f):
                pe.wait_ge(s_hid, NG * (f + 1))
                pe.wait_ge(s_ranked, NG * (f + 1))
                pe.wait_ge(s_sum, NG * (f + 1))
                pe.wait_ge(s_tabd, 32 * (f + 1))
                pe.wait_ge(s_whi, WEIGHTS)
                pe.wait_ge(s_wlo, WEIGHTS)
                words = {}

                def step(u, q, i):
                    done = f * TILES
                    if i == 0:
                        words.clear()
                    if tile := back(u, q, i, 0):
                        t, round_, r = tile
                        pe.wait_ge(c_in[r], (round_ + f * NQ + 1) * 16)
                        wait(pe, c_hi, t + done - 1)
                        wait(pe, c_lo, t + done - 1)
                        for k in range(KC):
                            last = pe.transpose(pT[:, r % 2, k * P:(k + 1) * P], tile_in[r][:, k * P:(k + 1) * P],
                                                ident[:])
                        last.then_inc(c_xt, 1)
                    if tile := back(u, q, i, UP_LAG):
                        t, _, r = tile
                        e = expert_in(words, q, (i - UP_LAG) // RING, r)
                        pe.wait_ge(c_hi, t + done + 1)
                        pe.wait_ge(c_lo, t + done + 1)
                        wait(pe, c_hid, t + done - 1)
                        last = project(p_tile_up[r % 2],
                                       [(cols(tile_x[r % 2], k * P, P),
                                         tuple(w[:, bass.ds(e * (KC * HU) + k * HU, HU)] for w in up_e))
                                        for k in range(KC)])
                        last.then_inc(c_up, 1)
                    if tile := back(u, q, i, HT_LAG):
                        t, _, r = tile
                        pe.wait_ge(c_hid, t + done + 1)
                        wait(pe, c_hidhi, t + done - 1)
                        wait(pe, c_hidlo, t + done - 1)
                        pe.transpose(p_tile_ht[r % 2], tile_hid[r % 2], ident[:]).then_inc(c_ht, 1)
                    if tile := back(u, q, i, DOWN_LAG):
                        t, _, r = tile
                        e = expert_in(words, q, (i - DOWN_LAG) // RING, r)
                        pe.wait_ge(c_hidhi, t + done + 1)
                        pe.wait_ge(c_hidlo, t + done + 1)
                        wait(pe, c_out, t + done - 1)
                        last = project(pO[:, r % 2, 0:D],
                                       [(tile_hidp[r % 2], tuple(w[:, bass.ds(e * D, D)] for w in down_e))])
                        last.then_inc(c_down, 1)

                def expert_in(words, q, offset, r):
                    key = (offset, r // 4)
                    if key not in words:
                        at = ((q + offset) * (RING // 4) + r // 4) * TAB + 4
                        words[key] = pe.value_load(tab_row[0:1, bass.ds(at, 1)], min_val=0, max_val=E ** 4 - 1)
                    return (words[key] // (E ** (r % 4))) % E

                all_tiles(pe, step, DOWN_LAG)

            def w_in_chunk(g, f):
                c = g * FC
                if f == 0:
                    wait(pe, s_hid, g + NG - 1)
                    wait(pe, m_tap0, c)
                elif f == 1:
                    pe.wait_ge(s_ranked, g + NG - 1)
                    wait(pe, m_sz, c)
                elif f == 2:
                    pe.wait_ge(m_tap0, c + 1)
                    pe.wait_ge(m_sz, c + 1)
                else:
                    pe.wait_ge(m_sz, c + 3)
                    wait(pe, s_logit, g + NG)
                for h in range(2):
                    last = project(p_mix[f][h], [(cols(win, k * 2 * M + h * M + f * P, P), cols(xt[0], k * GT, GT))
                                                 for k in range(KC)])
                last.then_inc(m_win, 1)

            def w_out_chunk(g, f):
                if f == 0:
                    wait(pe, m_x3, g)
                pe.wait_ge(m_mix, g * FC + f + 1)
                for i in range(G):
                    last = pe.matmul(pO[:, i // 2, (i % 2) * D:(i % 2 + 1) * D], conv[f][:, i * P:(i + 1) * P],
                                     wout[:, f * D:(f + 1) * D], start=(f == 0 and i % 2 == 0),
                                     stop=(f == FC - 1), skip_group_check=True)
                last.then_inc(m_wout, 1)

            def mix_groups(g, j, b):
                prev, after = neighbours(g, j, b)
                here = not (isinstance(g, int) and g >= NG)
                if here:
                    pe.wait_ge(s_xthi, mixer_norm(g) + 1)
                    pe.wait_ge(s_xtlo, mixer_norm(g) + 1)
                    w_in_chunk(g, 0)
                    w_in_chunk(g, 1)
                if prev:
                    turn(ffn_norm(prev[0]), norm[1], lambda: wait(pe, s_sum, g + NG - 1))
                if here:
                    w_in_chunk(g, 2)
                if prev:
                    pe.wait_ge(m_sz, g * FC)
                    if here:
                        pe.wait_ge(m_tap0, g * FC + 3)
                        pe.wait_ge(m_sz, g * FC + 2)
                    gate_and_up(prev[0] + NG, ffn_norm(prev[0]), xt[1])
                if here:
                    w_out_chunk(g, 0)
                    w_in_chunk(g, 3)
                    w_out_chunk(g, 1)
                if prev:
                    ranks(prev[0] + NG)
                    down(prev[0] + NG, pT)
                if here:
                    w_out_chunk(g, 2)
                if after:
                    turn(mixer_norm(after[0]), norm[0], lambda: wait(pe, s_sum, g + NG))
                if here:
                    w_out_chunk(g, 3)

            pe.wait_ge(s_const, CONSTS)
            turn(0, norm[0], lambda: None)
            pe.wait_ge(s_whi, LOADS_A)
            pe.wait_ge(s_wlo, LOADS_A)
            pe.wait_ge(s_half_w, 1)
            all_groups(pe, route_groups)
            tiles(0)
            pe.wait_ge(c_out, TILES)
            pe.wait_ge(s_small, 64)
            turn(NG, norm[0], lambda: None)
            all_groups(pe, mix_groups)
            mix_groups(NG, NP, 0)
            tiles(1)

        @block.vector
        def _(dve):
            def split_low(i):
                pair, at, cols, scale, _ = loads[i]
                dve.wait_ge(s_whi, i + 1)
                dve.scalar_tensor_tensor(pair[1][:, at:at + cols], stage[i % 2][:, 0:cols], scale,
                                         pair[0][:, at:at + cols], ALU.mult, ALU.subtract).then_inc(s_wlo, 1)

            def split_low_experts(j, b):
                dve.wait_ge(s_whi, j * 2 + b + len(loads) + 1)
                dst, cols, scale = ((up_e, UP2, 1.0), (down_e, DOWN2, 0.5))[b]
                dve.scalar_tensor_tensor(dst[1][:, bass.ds(j * cols, cols)], stage[b][:, 0:cols], scale,
                                         dst[0][:, bass.ds(j * cols, cols)], ALU.mult, ALU.subtract)\
                   .then_inc(s_wlo, 1)

            def statistics(m, src):
                wait(dve, s_norm, m)
                for i in range(G):
                    last = dve.bn_stats(stats[:, i, :], src[:, i, :])
                last.then_inc(s_stats, 1)
                dve.wait_ge(s_stats, m + 1)
                dve.sem_inc(s_passed_dve, 1)
                for i in range(G):
                    last = dve.bn_aggr(mean_var[:, i, :], stats[:, i, :])
                last.then_inc(s_aggr, 1)
                dve.wait_ge(s_aggr, m + 1)
                dve.tensor_scalar(var_eps[:], mean_var[:, :, 1], EPS, None, ALU.add).then_inc(s_vareps, 1)

            def base_affine(n, m):
                dve.wait_ge(s_rstd, m + 1)
                wait(dve, s_base, n)
                dve.tensor_scalar(base_scale[:], rstd[:], 0.5, 1.0, ALU.mult, ALU.add)
                dve.scalar_tensor_tensor(base_shift[:], mean_var[:, :, 0], -0.5, rstd[:], ALU.mult, ALU.mult)\
                   .then_inc(s_shift, 1)

            def normalise(m, src, dst, free):
                dve.wait_ge(s_rstd, m + 1)
                free()
                for i in range(G):
                    last = dve.tensor_scalar(dst[:, i, :], src[:, i, :], mean_var[:, i, 0:1], rstd[:, i:i + 1],
                                             ALU.subtract, ALU.mult)
                last.then_inc(s_norm, 1)

            def x_low(m, dst):
                dve.wait_ge(s_xthi, m + 1)
                for k in range(KC):
                    last = dve.tensor_tensor(dst[1][:, k * GT:(k + 1) * GT], pT[:, k, :],
                                             dst[0][:, k * GT:(k + 1) * GT], ALU.subtract)
                last.then_inc(s_xtlo, 1)

            def choose(f, g):
                n = g + f * NG
                k = [0]

                def then(ins):
                    k[0] += 1
                    ins.then_inc(s_route, 1)
                    dve.wait_ge(s_route, n * (CHOOSE_STEPS + PLACE_STEPS) + k[0])

                dve.wait_ge(s_gate, n + 1)
                dve.tensor_tensor(logit[:], p_gate, gate_bias[:].unsqueeze(1).to_broadcast([P, G, E]), ALU.add)\
                   .then_inc(s_logit, 1)
                dve.wait_ge(s_logit, n + 1)
                then(dve.tensor_scalar(logit[:], logit[:], SATURATED, None, ALU.min))
                dve.sem_inc(s_passed_dve, 1)
                for i in range(G):
                    last = dve.max(best[:, i, :], logit[:, i, :])
                then(last)
                dve.sem_inc(s_passed_dve, 1)
                for i in range(G):
                    last = dve.max_index(best_at[:, i, :], best[:, i, :], logit[:, i, :])
                then(last)
                dve.tensor_copy(logit_of[:, bass.ds(g * G * K, G * K)].rearrange("p (i k) -> p i k", k=K),
                                best[:, :, 0:K])
                then(dve.tensor_copy(chosen[:].rearrange("p (i k) -> p i k", k=K), best_at[:, :, 0:K]))
                then(dve.tensor_tensor(onehot[:], chosen[:].unsqueeze(2).to_broadcast([P, G * K, E]),
                                       expert_ids[:].unsqueeze(1).to_broadcast([P, G * K, E]), ALU.is_equal))
                wait(dve, s_rank, n)
                dve.tensor_tensor(members[:], onehot[:, 0::K, :], onehot[:, 1::K, :], ALU.add).then_inc(s_members, 1)
                dve.tensor_copy(expert_of[:, bass.ds(g * G * K, G * K)], chosen[:])
                assert k[0] == CHOOSE_STEPS

            def place(f, g, j, b):
                n = g + f * NG
                k = [CHOOSE_STEPS]

                def then(ins):
                    k[0] += 1
                    ins.then_inc(s_route, 1)
                    dve.wait_ge(s_route, n * (CHOOSE_STEPS + PLACE_STEPS) + k[0])

                dve.wait_ge(s_rank, n + 1)
                then(dve.tensor_tensor(rank_all[:], p_rank, counts[:, f, :].unsqueeze(1).to_broadcast([P, G, E]),
                                       ALU.add))
                dve.tensor_tensor(counts[:, f, :], counts[:, f, :], p_total, ALU.add).then_inc(s_ranked, 1)
                then(dve.tensor_tensor(rank_pick[:].rearrange("p (i k) e -> p i k e", k=K),
                                       onehot[:].rearrange("p (i k) e -> p i k e", k=K),
                                       rank_all[:].unsqueeze(2).to_broadcast([P, G, K, E]), ALU.mult))
                then(dve.tensor_reduce(rank[:], rank_pick[:], AX.X, ALU.add))
                dve.tensor_copy(rank_of[:, bass.ds(g * G * K, G * K)], rank[:])
                then(dve.tensor_copy(rank_i[:], rank[:]))
                dve.tensor_scalar(slot_row[:], rank_i[:], P - 1, (E * COLS).bit_length() - 1,
                                  ALU.bitwise_and, ALU.logical_shift_left)
                then(dve.tensor_scalar(slot_col[:], rank_i[:], P.bit_length() - 1, None, ALU.logical_shift_right))
                then(dve.scalar_tensor_tensor(slot_ec[:], chosen[:], float(COLS), slot_col[:], ALU.mult, ALU.add))
                wait(dve, s_scat[b], (j + f * NP) * SCAT)
                dve.tensor_tensor(slot[b][:], slot_ec[:], slot_row[:], ALU.add).then_inc(s_slot, 1)
                assert k[0] == CHOOSE_STEPS + PLACE_STEPS

            CHOOSE_STEPS, PLACE_STEPS = 5, 6

            def shared_hidden(n):
                dve.wait_ge(s_silu, n + 1)
                wait(dve, s_down, n)
                dve.tensor_tensor(hid[:], silu_g[:], p_up[1], ALU.mult).then_inc(s_hid, 1)

            def make_sum(n, b, src):
                dve.wait_ge(s_down, n + 1)
                dve.wait_ge(s_base, n + 1)
                for h in range(2):
                    half = base[b][:, 2 * h:2 * h + 2, :].rearrange("p i d -> p (i d)")
                    last = dve.tensor_tensor(half, src[:, h, :], half, ALU.add)
                last.then_inc(s_sum, 1)

            def start_norm(g, j, b):
                dve.wait_ge(s_rows[b], (j + 1) * 16)
                statistics(g, rows[b])

            def end_norm(g, j, b):
                def free():
                    wait(dve, s_xt, g - 1)
                    wait(dve, s_normed[b], j * 16)

                base_affine(g, g)
                normalise(g, rows[b], norm[b], free)

            def route_groups(g, j, b):
                _, after = neighbours(g, j, b)
                if after:
                    start_norm(*after)
                choose(0, g)
                if after:
                    end_norm(*after)
                shared_hidden(g)
                place(0, g, j, b)
                if after:
                    x_low(after[0], xt[after[2]])
                split_low_experts(j, b)
                make_sum(g, b, pO)

            def plan(f):
                k = [0]

                def then(ins):
                    k[0] += 1
                    ins.then_inc(s_plan, 1)
                    dve.wait_ge(s_plan, f * PLAN_STEPS + k[0])

                dve.wait_ge(s_ranked, NG * (f + 1))
                then(dve.tensor_scalar(tiles_i[:], counts[:, f, :], float(P - 1), None, ALU.add))
                then(dve.tensor_scalar(tiles_i[:], tiles_i[:], P.bit_length() - 1, None, ALU.logical_shift_right))
                then(dve.tensor_copy(tiles_f[:], tiles_i[:]))
                then(dve.tensor_tensor_scan(tiles_upto[:], ones_e[:], tiles_f[:], 0.0, ALU.mult, ALU.add))
                then(dve.tensor_tensor(passed[:], tile_ids[:].unsqueeze(2).to_broadcast([P, 4, E]),
                                       tiles_upto[:].unsqueeze(1).to_broadcast([P, 4, E]), ALU.is_ge))
                then(dve.tensor_tensor(passed_n[:], passed[:], tiles_f[:].unsqueeze(1).to_broadcast([P, 4, E]),
                                       ALU.mult))
                dve.tensor_reduce(tab_e[:], passed[:], AX.X, ALU.add)
                then(dve.tensor_reduce(tab_s[:], passed_n[:], AX.X, ALU.add))
                then(dve.tensor_scalar(tab_e[:], tab_e[:], float(E - 1), None, ALU.min))
                then(dve.tensor_tensor(tab_s[:], tile_ids[:], tab_s[:], ALU.subtract))
                then(dve.scalar_tensor_tensor(tab_s[:], tab_e[:], float(COLS), tab_s[:], ALU.mult, ALU.add))
                for c in (2, 1, 0):
                    high = tab_e[:, 3:4] if c == 2 else tab_pack[:, c + 1:c + 2]
                    then(dve.scalar_tensor_tensor(tab_pack[:, c:c + 1], high, float(E), tab_e[:, c:c + 1],
                                                  ALU.mult, ALU.add))
                wait(dve, s_tabd, 32 * f)
                dve.tensor_copy(tab_i[:, 4:5], tab_pack[:, 0:1])
                dve.tensor_scalar(tab_i[:, 0:4], tab_s[:], float(E * COLS - 1), None, ALU.min).then_inc(s_tab, 1)
                then(dve.tensor_tensor(first_row[:], tiles_upto[:], tiles_f[:], ALU.subtract))
                then(dve.tensor_scalar(first_row[:], first_row[:], float(P), None, ALU.mult))
                wide = rows[0][:].rearrange("p i (c e) -> p (i c) e", e=E)
                half = NT * K // 2
                dve.wait_ge(s_base, NG * (f + 1))
                for h in range(2):
                    part = slice(h * half, (h + 1) * half)
                    then(dve.tensor_tensor(wide, expert_of[:, part].unsqueeze(2).to_broadcast([P, half, E]),
                                           expert_ids[:].unsqueeze(1).to_broadcast([P, half, E]), ALU.is_equal))
                    then(dve.tensor_tensor(wide, wide, first_row[:].unsqueeze(1).to_broadcast([P, half, E]),
                                           ALU.mult))
                    then(dve.tensor_reduce(expert_of[:, part], wide, AX.X, ALU.add))
                then(dve.tensor_tensor(position[:], expert_of[:], rank_of[:], ALU.add))
                dve.wait_ge(s_exp, f + 1)
                then(dve.tensor_scalar(exp_neg, exp_neg, 1.0, None, ALU.add))
                then(dve.tensor_tensor(denom[:], exp_neg[:, :, 0], exp_neg[:, :, 1], ALU.add))
                then(dve.reciprocal(denom[:], denom[:]))
                dve.tensor_tensor(weight[:, :, 0], exp_neg[:, :, 1], denom[:], ALU.mult)
                dve.tensor_tensor(weight[:, :, 1], exp_neg[:, :, 0], denom[:], ALU.mult).then_inc(s_pos, 1)
                assert k[0] == PLAN_STEPS

            PLAN_STEPS = 25

            def tiles(f):
                dve.wait_ge(s_down, NG * (f + 1))

                def step(u, q, i):
                    done = f * TILES
                    if tile := back(u, q, i, 0):
                        t, _, r = tile
                        dve.wait_ge(c_hi, t + done + 1)
                        dve.tensor_tensor(tile_x[r % 2][1], pT[:, r % 2, 0:D], tile_x[r % 2][0], ALU.subtract)\
                           .then_inc(c_lo, 1)
                    if tile := back(u, q, i, UP_LAG):
                        t, _, r = tile
                        dve.wait_ge(c_silu, t + done + 1)
                        wait(dve, c_ht, t + done - 1)
                        dve.tensor_tensor(tile_hid[r % 2], tile_silu[r % 2], p_tile_up[r % 2][:, H:HU], ALU.mult)\
                           .then_inc(c_hid, 1)
                    if tile := back(u, q, i, HT_LAG):
                        t, _, r = tile
                        dve.wait_ge(c_hidhi, t + done + 1)
                        dve.tensor_tensor(tile_hidp[r % 2][1], p_tile_ht[r % 2], tile_hidp[r % 2][0], ALU.subtract)\
                           .then_inc(c_hidlo, 1)

                all_tiles(dve, step, HT_LAG)

            def combine(f, g, j, b):
                n = g + f * NG
                wait(dve, m_comb, n)
                dve.tensor_copy(weight_now[:].rearrange("p (i k) -> p i k", k=K), weight[:, bass.ds(g * G, G), :])\
                   .then_inc(m_weight, 1)
                dve.wait_ge(s_rows[b], (j + (f + 1) * NP + 1) * 16)
                dve.wait_ge(m_picked[b], (j + f * NP + 1) * SCAT)
                dve.wait_ge(m_weight, n + 1)
                for k in range(K):
                    for i in range(G):
                        last = dve.scalar_tensor_tensor(rows[b][:, i, :], picked_in[b * f][i][k],
                                                        weight_now[:, i * K + k:i * K + k + 1], rows[b][:, i, :],
                                                        ALU.mult, ALU.add)
                    last.then_inc(m_add if k == 0 else m_comb, 1)
                    if k == 0:
                        dve.wait_ge(m_add, n + 1)

            def start_mixer(g, j, b):
                combine(0, g, j, b)
                dve.wait_ge(m_comb, g + 1)
                statistics(mixer_norm(g), rows[b])

            def end_mixer_norm(g, j, b):
                def free():
                    if not (isinstance(g, int) and g == 0):
                        dve.wait_ge(s_xt, mixer_norm(g - 1) + 1)

                normalise(mixer_norm(g), rows[b], norm[0], free)

            def other_taps(g, f, b):
                c = g * FC + f
                i = f % 2
                wait(dve, m_tap, (c - 1) * T3)
                if b == 0:
                    dve.memset(xc[i][:, 0:T3], 0.0).then_inc(m_halo, 1)
                    dve.wait_ge(m_xc, c + 1)
                    dve.tensor_copy(halo[:, f, :], xc[i][:, GT:GT + T3]).then_inc(m_halo, 1)
                else:
                    dve.tensor_copy(xc[i][:, 0:T3], halo[:, f, :]).then_inc(m_halo, 2)
                    dve.wait_ge(m_xc, c + 1)
                dve.wait_ge(m_halo, (c + 1) * 2)
                dve.wait_ge(m_tap0, c + 1)
                for k in range(T3):
                    if k:
                        dve.wait_ge(m_tap, c * T3 + k)
                    dve.scalar_tensor_tensor(conv[f][:], xc[i][:, k:k + GT], taps[:, f, k:k + 1], conv[f][:],
                                             ALU.mult, ALU.add).then_inc(m_tap, 1)

            def mix(g, f):
                c = g * FC + f
                dve.wait_ge(m_xa, c + 1)
                dve.wait_ge(m_sz, c + 1)
                dve.tensor_tensor(conv[f][:], conv[f][:], silu_z[f % 2][:], ALU.mult).then_inc(m_mix, 1)

            def end_mixer(g, b):
                dve.wait_ge(m_wout, (g + 1) * FC)
                for h in range(2):
                    half = rows[b][:, 2 * h:2 * h + 2, :].rearrange("p i d -> p (i d)")
                    last = dve.tensor_tensor(half, pO[:, h, :], half, ALU.add)
                last.then_inc(m_x3, 1)
                dve.wait_ge(m_x3, g + 1)

            def mix_groups(g, j, b):
                prev, after = neighbours(g, j, b)
                here = not (isinstance(g, int) and g >= NG)
                if prev:
                    pg, pj, pb = prev
                    end_mixer(pg, pb)
                    statistics(ffn_norm(pg), rows[pb])
                if here:
                    other_taps(g, 0, b)
                if prev:
                    def norm1_free():
                        if not (isinstance(pg, int) and pg == 0):
                            dve.wait_ge(s_xt, ffn_norm(pg - 1) + 1)
                        dve.wait_ge(s_normed[1 - pb], (pj + NP + pb) * 16)

                    base_affine(pg + NG, ffn_norm(pg))
                    normalise(ffn_norm(pg), rows[pb], norm[1], norm1_free)
                if here:
                    other_taps(g, 1, b)
                if prev:
                    x_low(ffn_norm(pg), xt[1])
                if here:
                    mix(g, 0)
                if prev:
                    choose(1, pg)
                if here:
                    other_taps(g, 2, b)
                    mix(g, 1)
                if prev:
                    shared_hidden(pg + NG)
                if after:
                    start_mixer(*after)
                if here:
                    other_taps(g, 3, b)
                    mix(g, 2)
                if prev:
                    place(1, *prev)
                if after:
                    end_mixer_norm(*after)
                if prev:
                    make_sum(pg + NG, pb, pT)
                if here:
                    mix(g, 3)
                if after:
                    x_low(mixer_norm(after[0]), xt[0])

            dve.memset(counts[:], 0.0).then_inc(s_zero, 1)
            dve.wait_ge(s_zero, 1)
            start_norm(0, 0, 0)
            split_low(0)
            split_low(1)
            end_norm(0, 0, 0)
            x_low(0, xt[0])
            for i in range(2, len(loads)):
                split_low(i)
            dve.wait_ge(s_const, CONSTS)
            dve.wait_ge(s_small, 64)
            all_groups(dve, route_groups)
            plan(0)
            tiles(0)
            dve.wait_ge(c_xt, TILES)
            dve.wait_ge(c_ht, TILES)
            start_mixer(0, 0, 0)
            end_mixer_norm(0, 0, 0)
            x_low(NG, xt[0])
            all_groups(dve, mix_groups)
            mix_groups(NG, NP, 0)
            plan(1)
            tiles(1)
            dve.wait_ge(c_xt, 2 * TILES)
            all_groups(dve, lambda g, j, b: combine(1, g, j, b))


_INS = ["x", "w_in", "w_conv", "b_conv", "w_out"]
_FFN = ["gate_w", "gate_b", "shared_wg", "shared_wu", "shared_wd", "experts_wg", "experts_wu", "experts_wd"]


def kernel(**inputs):
    import numpy as np
    import concourse.bacc as bacc
    from concourse.bass_utils import run_bass_kernel_spmd

    nc = bacc.Bacc("TRN2", target_bir_lowering=False, num_devices=1)
    arrays, args = {}, []
    for name in [f"L0_attn_{n}" for n in _INS] + [f"L0_ffn_{n}" for n in _FFN]:
        a = np.ascontiguousarray(inputs[name])
        arrays[f"in_{name}"] = a
        args.append(nc.dram_tensor(f"in_{name}", a.shape, mybir.dt.from_np(a.dtype), kind="ExternalInput").ap())
    shape = inputs["L0_attn_x"].shape
    args.append(nc.dram_tensor("out_0", shape, F32, kind="ExternalOutput").ap())
    build_macaron(nc, *args)
    r = run_bass_kernel_spmd(nc, [arrays], core_ids=[0])
    return r.results[0]["out_0"]
```

```python
from contextlib import ExitStack

import concourse.bass as bass
from concourse import mybir
from concourse.alu_op_type import AluOpType as ALU

ACT = mybir.ActivationFunctionType
AX = mybir.AxisListType
F32 = mybir.dt.float32
F32R = mybir.dt.float32r
BF16 = mybir.dt.bfloat16
I32 = mybir.dt.int32
U32 = mybir.dt.uint32

P = 128
G = 4
GT = G * P
EPS = 1e-5
SATURATED = 17.33


def wait(engine, semaphore, value):
    if not (isinstance(value, int) and value <= 0):
        engine.wait_ge(semaphore, value)


def build_macaron(nc, x, w_in, w_conv, b_conv, w_out, gate_w, gate_b, shared_wg, shared_wu, shared_wd,
                  experts_wg, experts_wu, experts_wd, out):
    B, L, D = x.shape
    T = B * L
    E, _, H = experts_wg.shape
    M = w_out.shape[0]
    TAPS = w_conv.shape[2]
    K = 2
    KC = D // P
    FC = M // P
    NT = T // P
    NG = T // GT
    NP = NG // 2
    HU = 2 * H
    RING = 12
    BUFS = 6
    PACK = 6
    TILES = -(-(T * K // P + E - 1) // RING) * RING
    COLS = T // P
    assert D == 256 and H == P and L == 2 * GT and M == FC * P and E == 16 and TILES <= 2 * P and G * D == E * T // P

    x_rows = x.rearrange("b l d -> (b l) d")
    out_rows = out.rearrange("b l d -> (b l) d")

    def grouped(rows):
        return rows.rearrange("(i p) d -> p i d", p=P)

    normed = [nc.dram_tensor(f"normed{f}", (T, D), F32).ap() for f in range(2)]
    sums = [nc.dram_tensor(f"sums{f}", (T, D), F32).ap() for f in range(2)]
    expert_out = [nc.dram_tensor(f"expert_out{f}", (TILES * P, D), F32).ap() for f in range(2)]
    lists = [nc.dram_tensor(f"lists{f}", (E * T, 1), F32).ap() for f in range(2)]
    tables = [nc.dram_tensor(f"tables{f}", (P, 1), I32).ap() for f in range(2)]

    with ExitStack() as ctx:
        def sb(name, shape, dt=F32):
            return ctx.enter_context(nc.sbuf_tensor(name, shape, dt))

        def sem(name):
            return ctx.enter_context(nc.semaphore(name))

        def parts(name, shape):
            return sb(name + "_hi", shape, F32R), sb(name + "_lo", shape, F32R)

        gate = parts("gate", [P, KC * E])
        up_s = parts("up_s", [P, KC * HU])
        up_e = parts("up_e", [P, E * KC * HU])
        down_e = parts("down_e", [P, E * D])
        win = parts("win", [P, KC * 2 * M])
        down_s = sb("down_s", [P, D])
        wout = sb("wout", [P, FC * D])
        taps = sb("taps", [P, FC, TAPS])
        conv_bias = sb("conv_bias", [P, FC])
        gate_bias = sb("gate_bias", [P, E])

        ident = sb("ident", [P, P])
        before = sb("before", [P, P], BF16)
        ones = sb("ones", [P, P], BF16)
        expert_ids = sb("expert_ids", [P, E])
        tile_ids = sb("tile_ids", [P, PACK + 2])
        ones_e = sb("ones_e", [P, E])
        minus_half = sb("minus_half", [P, G])
        token_ids = sb("token_ids", [P, NT])

        rows = [sb(f"rows{b}", [P, G, D]) for b in range(2)]
        sum_in = sb("sum_in", [P, G, D])
        norm = [sb(f"norm{b}", [P, G, D]) for b in range(2)]
        base = [sb(f"base{b}", [P, G, D]) for b in range(2)]
        xt = [parts(f"xt{i}", [P, KC * GT]) for i in range(2)]
        silu_g = sb("silu_g", [P, GT])
        hid = sb("hid", [P, GT])
        picked = sb("picked", [P, G, K, D])
        xc = [sb(f"xc{i}", [P, GT + TAPS - 1]) for i in range(2)]
        halo = sb("halo", [P, FC, TAPS - 1])
        no_halo = sb("no_halo", [P, TAPS - 1])
        silu_z = [sb(f"silu_z{i}", [P, GT]) for i in range(2)]
        conv = [sb(f"conv{f}", [P, GT]) for f in range(FC)]
        hid_parts = parts("hid_parts", [P, 2 * P])

        stats = sb("stats", [P, G, 6])
        mean_var = sb("mean_var", [P, G, 2])
        var_eps = sb("var_eps", [P, G])
        rstd = sb("rstd", [P, G])
        norm_shift = sb("norm_shift", [P, G])
        base_scale = sb("base_scale", [P, G])
        base_shift = sb("base_shift", [P, G])
        logit = sb("logit", [P, G, E])
        best = sb("best", [P, G, 8])
        best_at = sb("best_at", [P, G, 8], U32)
        chosen = sb("chosen", [P, G * K])
        onehot = sb("onehot", [P, G * K, E])
        members = sb("members", [P, G, E], BF16)
        rank_all = sb("rank_all", [P, G, E])
        rank_pick = sb("rank_pick", [P, G * K, E])
        rank = sb("rank", [P, G * K])
        slot = [sb(f"slot{b}", [P, G * K], U32) for b in range(2)]
        token = [sb(f"token{b}", [P, G]) for b in range(2)]
        counts = sb("counts", [P, 2, E])
        expert_of = sb("expert_of", [P, NT * K])
        rank_of = sb("rank_of", [P, NT * K])
        logit_of = sb("logit_of", [P, NT * K])
        position = sb("position", [P, NT * K], I32)
        weight = sb("weight", [P, NT, K])
        exp_neg = logit_of[:].rearrange("p (t k) -> p t k", k=K)
        denom = sb("denom", [P, NT])
        tiles_i = sb("tiles_i", [P, E], I32)
        tiles_f = sb("tiles_f", [P, E])
        tiles_upto = sb("tiles_upto", [P, E])
        first_row = sb("first_row", [P, E])
        passed = sb("passed", [P, PACK + 2, E])
        passed_n = sb("passed_n", [P, PACK + 2, E])
        tab_e = sb("tab_e", [P, PACK + 2])
        tab_s = sb("tab_s", [P, PACK + 2])
        tab_pack = sb("tab_pack", [P, PACK])
        tab_i = sb("tab_i", [P, 1], I32)
        tab_row = sb("tab_row", [1, TILES // PACK], I32)
        list_at = sb("list_at", [P, 2], U32)
        list_rows = sb("list_rows", [P, 2, P])
        tokens_of = sb("tokens_of", [P, TILES], U32)
        gather_at = sb("gather_at", [P, RING], U32)
        weight_now = sb("weight_now", [P, G * K])
        pick_at = [sb(f"pick_at{b}", [P, G * K], U32) for b in range(2)]

        pT = ctx.enter_context(nc.psum_tensor("pT", [P, 2, 512], F32))
        pR = ctx.enter_context(nc.psum_tensor("pR", [P, 4, 512], F32))
        pO = ctx.enter_context(nc.psum_tensor("pO", [P, 2, 512], F32))
        p_gate = pT[:, 0, 0:G * E].rearrange("p (i e) -> p i e", i=G)
        p_up = (pR[:, 3, :], pR[:, 0, :])
        p_rank = pR[:, 3, 0:G * E].rearrange("p (i e) -> p i e", i=G)
        p_total = pR[:, 3, G * E:G * E + E]
        p_mix = [(pR[:, (f % 2) * 2, :], pR[:, (f % 2) * 2 + 1, :]) for f in range(FC - 1)]
        p_mix.append((pR[:, 1, :], pR[:, 2, :]))

        clear = sum_in[:].rearrange("p i d -> p (i d)")
        tile_in = [norm[i // 4][:, i % 4, :] for i in range(BUFS)]
        tile_x = [tuple(t[:, c * D:(c + 1) * D] for t in xt[0]) for c in range(2)]
        tile_silu = [silu_g[:, c * H:(c + 1) * H] for c in range(2)]
        tile_hid = [hid[:, c * H:(c + 1) * H] for c in range(2)]
        tile_hidp = [tuple(t[:, c * P:(c + 1) * P] for t in hid_parts) for c in range(2)]
        tile_out = [base[i // 4][:, i % 4, :] for i in range(BUFS)]
        p_tile_up = [pR[:, c, 0:HU] for c in range(2)]
        p_tile_ht = [pR[:, 2 + c, 0:P] for c in range(2)]
        p_lists = pR[:, 3, 0:2 * P]
        picked_in = [[[picked[:, i, k, :] for k in range(K)] for i in range(G)],
                     [[norm[i // 2][:, (i % 2) * K + k, :] for k in range(K)] for i in range(G)]]

        stage = [picked[:, 2 * i:2 * i + 2, :, :].rearrange("p i k d -> p (i k d)") for i in range(2)]
        loads = []

        def piece(pair, at, cols, scale, *sources):
            loads.append((pair, at, cols, scale, sources))

        piece(gate, 0, KC * E, 1.0, (0, E, E, gate_w.rearrange("(k p) e -> p k e", p=P)))
        piece(up_s, 0, KC * HU, 1.0, (0, H, HU, shared_wg.rearrange("(k p) h -> p k h", p=P)),
              (H, H, HU, shared_wu.rearrange("(k p) h -> p k h", p=P)))
        LOADS_A = len(loads)
        win_view = w_in.rearrange("(k p) m -> p k m", p=P)
        for k in range(KC):
            piece(win, k * 2 * M, 2 * M, 1.0, (0, 2 * M, 2 * M, win_view[:, k:k + 1, :]))
        g_view = experts_wg.rearrange("e (k p) h -> p (e k) h", p=P)
        u_view = experts_wu.rearrange("e (k p) h -> p (e k) h", p=P)
        d_view = experts_wd.rearrange("e h d -> h e d")
        UP2, DOWN2 = 2 * KC * HU, 2 * D
        assert E == 2 * NP
        loaded = {0: 0, 1: 0}
        load_ready = []
        for i, (_, _, _, _, sources) in enumerate(loads):
            loaded[i % 2] += 16 * len(sources)
            load_ready.append(loaded[i % 2])

        s_const = sem("s_const")
        s_zero = sem("s_zero")
        s_small = sem("s_small")
        s_whole = sem("s_whole")
        s_half_w = sem("s_half_w")
        s_cleared = sem("s_cleared")
        s_stage = [sem("s_stage0"), sem("s_stage1")]
        s_whi = sem("s_whi")
        s_wlo = sem("s_wlo")
        s_passed_pool = sem("s_passed_pool")
        s_passed_dve = sem("s_passed_dve")
        s_rows = [sem("s_rows0"), sem("s_rows1")]
        s_stats = sem("s_stats")
        s_aggr = sem("s_aggr")
        s_vareps = sem("s_vareps")
        s_rstd = sem("s_rstd")
        s_shift = sem("s_shift")
        s_norm = sem("s_norm")
        s_base = sem("s_base")
        s_xt = sem("s_xt")
        s_xthi = sem("s_xthi")
        s_xtlo = sem("s_xtlo")
        s_gate = sem("s_gate")
        s_logit = sem("s_logit")
        s_up = sem("s_up")
        s_silu = sem("s_silu")
        s_hid = sem("s_hid")
        s_down = sem("s_down")
        s_sum = sem("s_sum")
        s_route = sem("s_route")
        s_members = sem("s_members")
        s_rank = sem("s_rank")
        s_ranked = sem("s_ranked")
        s_slot = sem("s_slot")
        s_token = sem("s_token")
        s_scat = [sem("s_scat0"), sem("s_scat1")]
        s_normed = [sem("s_normed0"), sem("s_normed1")]
        s_sums = [sem("s_sums0"), sem("s_sums1")]
        s_plan = sem("s_plan")
        s_tab = sem("s_tab")
        s_listat = sem("s_listat")
        s_list = sem("s_list")
        s_listt = sem("s_listt")
        s_tokens = sem("s_tokens")
        s_tabd = sem("s_tabd")
        s_exp = sem("s_exp")
        s_pos = sem("s_pos")
        c_at = sem("c_at")
        c_in = [sem(f"c_in{i}") for i in range(RING)]
        c_xt = sem("c_xt")
        c_hi = sem("c_hi")
        c_lo = sem("c_lo")
        c_up = sem("c_up")
        c_silu = sem("c_silu")
        c_hid = sem("c_hid")
        c_ht = sem("c_ht")
        c_hidhi = sem("c_hidhi")
        c_hidlo = sem("c_hidlo")
        c_down = sem("c_down")
        c_out = sem("c_out")
        c_stored = [sem(f"c_stored{i}") for i in range(RING)]
        m_at = sem("m_at")
        m_picked = [sem("m_picked0"), sem("m_picked1")]
        m_weight = sem("m_weight")
        m_add = sem("m_add")
        m_comb = sem("m_comb")
        m_win = sem("m_win")
        m_xc = sem("m_xc")
        m_tap0 = sem("m_tap0")
        m_sz = sem("m_sz")
        m_halo = sem("m_halo")
        m_tap = sem("m_tap")
        m_xa = sem("m_xa")
        m_mix = sem("m_mix")
        m_wout = sem("m_wout")
        m_x3 = sem("m_x3")
        s_out = [sem("s_out0"), sem("s_out1")]

        CONSTS = 12
        BETWEEN = 3
        SCAT = 16 * G * K
        NQ = TILES // RING
        UP_LAG, HT_LAG, DOWN_LAG = 1, 2, 3
        WEIGHTS = len(loads) + 2 * NP
        T3 = TAPS - 1
        block = ctx.enter_context(nc.Block())

        def split3(a, b):
            return [(a[0], b[0]), (a[0], b[1]), (a[1], b[0])]

        def mixer_norm(g):
            return NG if isinstance(g, int) and g == 0 else g * 2 + NG - 1

        def ffn_norm(g):
            return 3 * NG - 1 if isinstance(g, int) and g == NG - 1 else g * 2 + NG + 2

        def all_groups(engine, body):
            for b in range(2):
                body(b, 0, b)
            with engine.Fori(1, NP - 1) as j:
                for b in range(2):
                    body(j * 2 + b, j, b)
            for b in range(2):
                body(NG - 2 + b, NP - 1, b)

        def neighbours(g, j, b):
            before_g = None if isinstance(g, int) and g == 0 else (g - 1, j if b else j - 1, 1 - b)
            after_g = None if isinstance(g, int) and g >= NG - 1 else (g + 1, j + 1 if b else j, 1 - b)
            return before_g, after_g

        def all_tiles(engine, body, steps):
            for i in range(RING):
                body(i, 0, i)
            with engine.Fori(1, NQ) as q:
                for i in range(RING):
                    body(q * RING + i, q, i)
            for i in range(steps):
                body(TILES + i, NQ + i // RING, i % RING)

        def back(u, q, i, n):
            t = u - n
            if isinstance(t, int) and not 0 <= t < TILES:
                return None
            return t, q + (i - n) // RING, (i - n) % RING

        @block.sync
        def _(sp):
            def load_rows(src, n, b):
                sp.dma_start(rows[b][:], grouped(src[bass.ds(n * GT, GT), :])).then_inc(s_rows[b], 16)

            def load_sum(g, b):
                if not (isinstance(g, int) and g == 0):
                    sp.wait_ge(m_add, g)
                sp.dma_start(sum_in[:], grouped(sums[0][bass.ds(g * GT, GT), :])).then_inc(s_rows[b], 16)

            def load_piece(i):
                _, _, cols, _, sources = loads[i]
                if i >= 2:
                    sp.wait_ge(s_whi, i - 1)
                    sp.wait_ge(s_wlo, i - 1)
                for at, width, step, src in sources:
                    dst = stage[i % 2][:, 0:cols].rearrange("p (n s) -> p n s", s=step)[:, :, at:at + width]
                    sp.dma_start(dst, src).then_inc(s_stage[i % 2], 16)

            def load_experts(j, b):
                done = j * 2 + b + len(loads) - 1
                sp.wait_ge(s_whi, done)
                sp.wait_ge(s_wlo, done)
                if b == 0:
                    dst = stage[0].rearrange("p (n s) -> p n s", s=HU)
                    for h, view in enumerate((g_view, u_view)):
                        sp.dma_start(dst[:, :, h * H:(h + 1) * H], view[:, bass.ds(j * 2 * KC, 2 * KC), :])\
                            .then_inc(s_stage[0], 16)
                else:
                    sp.dma_start(stage[1][:, 0:DOWN2].rearrange("p (n d) -> p n d", d=D),
                                 d_view[:, bass.ds(j * 2, 2), :]).then_inc(s_stage[1], 16)

            def store_normed(f, g, b):
                sp.wait_ge(s_norm, (g if f == 0 else ffn_norm(g)) + 1)
                sp.dma_start(grouped(normed[f][bass.ds(g * GT, GT), :]), norm[b if f == 0 else 1][:])\
                    .then_inc(s_normed[b], 16)

            def store_sums(f, g, b):
                sp.wait_ge(s_sum, g + f * NG + 1)
                sp.dma_start(grouped(sums[f][bass.ds(g * GT, GT), :]), base[b][:]).then_inc(s_sums[b], 16)

            def route_groups(g, j, b):
                before_g, _ = neighbours(g, j, b)
                store_normed(0, g, b)
                sp.wait_ge(s_base, g + 1)
                last_pair = isinstance(g, int) and g >= NG - 2
                if not last_pair:
                    load_rows(x_rows, g + 2, b)
                if before_g:
                    store_sums(0, before_g[0], before_g[2])
                if not last_pair:
                    load_experts(j + 1, b)

            def mix_groups(g, j, b):
                before_g, _ = neighbours(g, j, b)
                if not (isinstance(g, int) and g >= NG - 2):
                    load_sum(g + 2, b)
                if before_g:
                    store_sums(1, before_g[0], before_g[2])
                store_normed(1, g, b)

            def tiles(f):
                sp.wait_ge(s_tab, f + 1)
                sp.dma_start(tables[f], tab_i[:]).then_inc(s_tabd, 16)
                sp.wait_ge(s_tabd, 32 * f + 16)
                if f:
                    sp.wait_ge(c_down, TILES)
                sp.dma_start(tab_row[:], tables[f][0:TILES // PACK, :].rearrange("(o p) c -> o (p c)", o=1))\
                    .then_inc(s_tabd, 16)

                def store(t, q, i):
                    sp.wait_ge(c_out, f * TILES + t + 1)
                    sp.dma_start(expert_out[f][bass.ds(t * P, P), :], tile_out[i % BUFS]).then_inc(c_stored[i], 16)

                all_tiles(sp, store, 0)

            load_piece(0)
            load_piece(1)
            for b in range(2):
                load_rows(x_rows, b, b)
            with nc.allow_non_contiguous_dma("small loads"):
                sp.dma_start(gate_bias[:], gate_b.partition_broadcast(P)).then_inc(s_small, 16)
                sp.dma_start(down_s[:], shared_wd).then_inc(s_whole, 16)
                for i in range(2, len(loads)):
                    load_piece(i)
                sp.wait_ge(s_const, CONSTS)
                for f in range(2):
                    sp.dma_start(lists[f].rearrange("(p c) o -> p (c o)", p=P), clear).then_inc(s_cleared, 16)
                sp.dma_start(taps[:], w_conv.rearrange("(f p) o t -> p f (o t)", p=P)).then_inc(s_small, 16)
                sp.dma_start(conv_bias[:], b_conv.rearrange("(f p) -> p f", p=P)).then_inc(s_small, 16)
                sp.dma_start(wout[:].rearrange("p (f d) -> p f d", d=D), w_out.rearrange("(f p) d -> p f d", p=P))\
                    .then_inc(s_small, 16)
            for b in range(2):
                load_experts(0, b)
            all_groups(sp, route_groups)
            store_sums(0, NG - 1, 1)
            tiles(0)
            for b in range(2):
                sp.wait_ge(s_sums[b], 16 * NP)
            for b in range(2):
                load_sum(b, b)
            all_groups(sp, mix_groups)
            store_sums(1, NG - 1, 1)
            tiles(1)
            for b in range(2):
                sp.wait_ge(s_sums[b], 32 * NP)
            for b in range(2):
                load_rows(sums[1], b, b)

            def store_out(g, j, b):
                sp.wait_ge(m_comb, NG + g + 1)
                sp.dma_start(grouped(out_rows[bass.ds(g * GT, GT), :]), rows[b][:]).then_inc(s_out[b], 16)
                sp.wait_ge(s_out[b], (j + 1) * 16)
                if not (isinstance(g, int) and g >= NG - 2):
                    load_rows(sums[1], g + 2, b)

            all_groups(sp, store_out)
            for b in range(2):
                sp.wait_ge(s_out[b], 16 * NP)

        @block.gpsimd
        def _(pool):
            pool.memset(ident[:], 0.0).then_inc(s_const, 1)
            pool.memset(before[:], 1.0).then_inc(s_const, 1)
            pool.memset(ones[:], 1.0).then_inc(s_const, 1)
            pool.memset(ones_e[:], 1.0).then_inc(s_const, 1)
            pool.memset(minus_half[:], -0.5).then_inc(s_const, 1)
            pool.memset(clear, 0.0).then_inc(s_const, 1)
            pool.iota(expert_ids[:], [[1, E]], base=0, channel_multiplier=0,
                      allow_small_or_imprecise_dtypes=True).then_inc(s_const, 1)
            pool.iota(tile_ids[:, 0:PACK], [[1, PACK]], base=0, channel_multiplier=PACK,
                      allow_small_or_imprecise_dtypes=True).then_inc(s_const, 1)
            pool.iota(tile_ids[:, PACK:PACK + 2], [[P, 2]], base=0, channel_multiplier=1,
                      allow_small_or_imprecise_dtypes=True).then_inc(s_const, 1)
            pool.iota(token_ids[:], [[P, NT]], base=0, channel_multiplier=1,
                      allow_small_or_imprecise_dtypes=True).then_inc(s_const, 1)
            pool.wait_ge(s_const, 10)
            pool.affine_select(out=ident[:], in_=ident[:], compare_op=ALU.not_equal, fill=1.0, base=0,
                               pattern=[[-1, P]], channel_multiplier=1).then_inc(s_const, 1)
            pool.affine_select(out=before[:], in_=before[:], compare_op=ALU.is_gt, fill=0.0, base=0,
                               pattern=[[1, P]], channel_multiplier=-1).then_inc(s_const, 1)

            def inverse_std(m):
                pool.wait_ge(s_vareps, m + 1)
                pool.tensor_tensor(rstd[:], var_eps[:], minus_half[:], ALU.pow).then_inc(s_rstd, 1)

            def scatter(f, g, b, between=lambda: None):
                n = g + f * NG
                pool.wait_ge(s_slot, n + 1)
                pool.tensor_copy(token[b][:], token_ids[:, bass.ds(g * G, G)]).then_inc(s_token, 1)
                pool.wait_ge(s_token, n + 1)
                pool.sem_inc(s_passed_pool, 1)
                for c in range(G * K):
                    if c == BETWEEN:
                        between()
                    pool.indirect_dma_start(lists[f], bass.IndirectOffsetOnAxis(slot[b][:, c:c + 1], 0),
                                            token[b][:, c // K:c // K + 1], None).then_inc(s_scat[b], 16)

            def gather_tiles(f):
                for b in range(2):
                    pool.wait_ge(s_normed[b], 16 * NP * (f + 1))
                pool.wait_ge(s_xt, NG * (1 + 2 * f))

                pool.wait_ge(s_listat, f + 1)
                for b in range(2):
                    pool.wait_ge(s_scat[b], SCAT * NP * (f + 1))
                wait(pool, s_listt, f)
                by_tile = lists[f].rearrange("(r p) o -> r (p o)", p=P)
                for h in range(2):
                    pool.indirect_dma_start(list_rows[:, h, :], None, by_tile,
                                            bass.IndirectOffsetOnAxis(list_at[:, h:h + 1], 0)).then_inc(s_list, 16)
                pool.wait_ge(s_tokens, f + 1)

                def gather(t, q, i):
                    wait(pool, c_xt, f * TILES + t - BUFS + 1)
                    if i % BUFS == 0:
                        pool.tensor_copy(gather_at[:, i:i + BUFS], tokens_of[:, bass.ds(t, BUFS)]).then_inc(c_at, 1)
                        pool.wait_ge(c_at, (f * NQ + q) * (RING // BUFS) + i // BUFS + 1)
                    pool.sem_inc(s_passed_pool, 1)
                    pool.indirect_dma_start(tile_in[i % BUFS], None, normed[f],
                                            bass.IndirectOffsetOnAxis(gather_at[:, i:i + 1], 0))\
                        .then_inc(c_in[i], 16)

                all_tiles(pool, gather, 0)

            def pick(f, g, b):
                wait(pool, m_comb, g if f == 0 else g + NG - 1)
                pool.tensor_copy(pick_at[b][:], position[:, bass.ds(g * G * K, G * K)]).then_inc(m_at, 1)
                pool.wait_ge(m_at, g + f * NG + 1)
                pool.sem_inc(s_passed_pool, 1)
                for c in range(G * K):
                    pool.indirect_dma_start(picked_in[b * f][c // K][c % K], None, expert_out[f],
                                            bass.IndirectOffsetOnAxis(pick_at[b][:, c:c + 1], 0))\
                        .then_inc(m_picked[b], 16)

            def wait_experts(f):
                pool.wait_ge(s_pos, f + 1)
                pool.wait_ge(c_xt, TILES * (f + 1))
                for i in range(RING):
                    pool.wait_ge(c_stored[i], 16 * NQ * (f + 1))

            def route_groups(g, j, b):
                last_pair = isinstance(g, int) and g >= NG - 2
                scatter(0, g, b, (lambda: None) if last_pair else (lambda: inverse_std(g + 2)))

            def mix_groups(g, j, b):
                before_g, after = neighbours(g, j, b)
                if before_g:
                    inverse_std(ffn_norm(before_g[0]))
                    if not (isinstance(g, int) and g < 2):
                        scatter(1, g - 2, b)
                if after:
                    inverse_std(mixer_norm(after[0]))
                    if not (isinstance(g, int) and g >= NG - 2):
                        pick(0, g + 2, b)

            inverse_std(0)
            inverse_std(1)
            pool.wait_ge(s_cleared, 32)
            all_groups(pool, route_groups)
            gather_tiles(0)
            wait_experts(0)
            pick(0, 0, 0)
            inverse_std(NG)
            pick(0, 1, 1)
            all_groups(pool, mix_groups)
            mix_groups(NG, NP, 0)
            scatter(1, NG - 1, 1)
            gather_tiles(1)
            wait_experts(1)
            all_groups(pool, lambda g, j, b: pick(1, g, b))

        @block.scalar
        def _(act):
            def split_high(i):
                pair, at, cols, scale, _ = loads[i]
                act.wait_ge(s_stage[i % 2], load_ready[i])
                act.activation(pair[0][:, at:at + cols], stage[i % 2][:, 0:cols], ACT.Copy, scale=scale)\
                   .then_inc(s_whi, 1)

            def split_high_experts(j, b):
                act.wait_ge(s_stage[b], (j + 1) * (32, 16)[b] + loaded[b])
                dst, cols, scale = ((up_e, UP2, 1.0), (down_e, DOWN2, 0.5))[b]
                act.activation(dst[0][:, bass.ds(j * cols, cols)], stage[b][:, 0:cols], ACT.Copy, scale=scale)\
                   .then_inc(s_whi, 1)

            def x_high(m, dst):
                act.wait_ge(s_xt, m + 1)
                for k in range(KC):
                    last = act.activation(dst[0][:, k * GT:(k + 1) * GT], pT[:, k, :], ACT.Copy)
                last.then_inc(s_xthi, 1)

            def normalise(m, src, dst, free):
                act.wait_ge(s_shift, m + 1)
                free()
                for i in range(G):
                    last = act.activation(dst[:, i, :], src[:, i, :], ACT.Identity, bias=norm_shift[:, i:i + 1],
                                          scale=rstd[:, i:i + 1])
                last.then_inc(s_norm, 1)

            def make_base(f, g, j, b):
                n = g + f * NG
                wait(act, s_sums[b], (j + f * NP) * 16)
                if f == 1 and isinstance(g, int) and g < 2:
                    for i in range(RING):
                        act.wait_ge(c_stored[i], 16 * NQ)
                for i in range(G):
                    last = act.activation(base[b][:, i, :], rows[b][:, i, :], ACT.Identity,
                                          bias=base_shift[:, i:i + 1], scale=base_scale[:, i:i + 1])
                last.then_inc(s_base, 1)

            def silu_shared(n):
                act.wait_ge(s_up, n + 1)
                wait(act, s_hid, n)
                act.activation(silu_g[:], p_up[0], ACT.Silu).then_inc(s_silu, 1)

            def route_groups(g, j, b):
                _, after = neighbours(g, j, b)
                if after:
                    norm_group(*after)
                silu_shared(g)
                if after:
                    x_high(after[0], xt[after[2]])
                split_high_experts(j, b)
                if after:
                    make_base(0, *after)

            def norm_group(g, j, b):
                def free():
                    wait(act, s_xt, g - 1)
                    wait(act, s_normed[b], j * 16)

                normalise(g, rows[b], norm[b], free)

            def mixer_norm_group(g, j, b):
                def free():
                    if not (isinstance(g, int) and g == 0):
                        act.wait_ge(s_xt, mixer_norm(g - 1) + 1)

                normalise(mixer_norm(g), rows[b], norm[0], free)

            def ffn_norm_group(g, j, b):
                def free():
                    if not (isinstance(g, int) and g == 0):
                        act.wait_ge(s_xt, ffn_norm(g - 1) + 1)
                    act.wait_ge(s_normed[1 - b], (j + NP + b) * 16)

                normalise(ffn_norm(g), rows[b], norm[1], free)

            def tiles(f):
                act.wait_ge(s_slot, NG * (f + 1))
                act.activation(logit_of[:], logit_of[:], ACT.Exp, scale=-1.0).then_inc(s_exp, 1)
                act.wait_ge(s_up, NG * (f + 1))
                act.wait_ge(s_hid, NG * (f + 1))
                for b in range(2):
                    act.wait_ge(s_sums[b], 16 * NP * (f + 1))
                wait(act, c_in[0], 16 * NQ * f)
                act.wait_ge(s_listt, f + 1)
                act.activation(tokens_of[:], p_lists[:, 0:TILES], ACT.Copy).then_inc(s_tokens, 1)

                def step(u, q, i):
                    done = f * TILES
                    if tile := back(u, q, i, 0):
                        t, _, r = tile
                        act.wait_ge(c_xt, t + done + 1)
                        wait(act, c_up, t + done - 1)
                        act.activation(tile_x[r % 2][0], pT[:, r % 2, 0:D], ACT.Copy).then_inc(c_hi, 1)
                    if tile := back(u, q, i, UP_LAG):
                        t, _, r = tile
                        act.wait_ge(c_up, t + done + 1)
                        wait(act, c_hid, t + done - 1)
                        act.activation(tile_silu[r % 2], p_tile_up[r % 2][:, 0:H], ACT.Silu).then_inc(c_silu, 1)
                    if tile := back(u, q, i, HT_LAG):
                        t, _, r = tile
                        act.wait_ge(c_ht, t + done + 1)
                        wait(act, c_down, t + done - 1)
                        act.activation(tile_hidp[r % 2][0], p_tile_ht[r % 2], ACT.Copy).then_inc(c_hidhi, 1)
                    if tile := back(u, q, i, DOWN_LAG):
                        t, round_, r = tile
                        act.wait_ge(c_down, t + done + 1)
                        wait(act, c_stored[r - BUFS], (round_ + (r >= BUFS) + f * NQ) * 16)
                        act.activation(tile_out[r % BUFS], pO[:, r % 2, 0:D], ACT.Copy).then_inc(c_out, 1)

                all_tiles(act, step, DOWN_LAG)

            def mix_chunk(g, f, j, b):
                c = g * FC + f
                act.wait_ge(m_win, c + 1)
                wait(act, m_tap, (c - 1) * T3)
                if b:
                    act.wait_ge(m_halo, j * FC + f + 1)
                act.activation(xc[f % 2][:, 0:T3], halo[:, f, :] if b else no_halo[:], ACT.Copy)
                act.activation(xc[f % 2][:, T3:], p_mix[f][0], ACT.Copy).then_inc(m_xc, 1)
                if not b:
                    wait(act, m_xc, c)
                    act.activation(halo[:, f, :], p_mix[f][0][:, GT - T3:GT], ACT.Copy).then_inc(m_halo, 1)
                wait(act, m_wout, c - 3)
                act.activation(conv[f][:], p_mix[f][0], ACT.Identity, bias=conv_bias[:, f:f + 1],
                               scale=taps[:, f, T3:TAPS]).then_inc(m_tap0, 1)
                wait(act, m_mix, c - 1)
                act.activation(silu_z[f % 2][:], p_mix[f][1], ACT.Silu).then_inc(m_sz, 1)

            def silu_conv(g, f):
                c = g * FC + f
                act.wait_ge(m_tap, (c + 1) * T3)
                act.activation(conv[f][:], conv[f][:], ACT.Silu).then_inc(m_xa, 1)

            def mix_groups(g, j, b):
                prev, after = neighbours(g, j, b)
                here = not (isinstance(g, int) and g >= NG)
                if here:
                    mix_chunk(g, 0, j, b)
                    mix_chunk(g, 1, j, b)
                if prev:
                    ffn_norm_group(*prev)
                if here:
                    silu_conv(g, 0)
                    mix_chunk(g, 2, j, b)
                if prev:
                    wait(act, s_up, prev[0] + NG)
                    x_high(ffn_norm(prev[0]), xt[1])
                if here:
                    silu_conv(g, 1)
                if prev:
                    make_base(1, *prev)
                if here:
                    mix_chunk(g, 3, j, b)
                if prev:
                    silu_shared(prev[0] + NG)
                if here:
                    silu_conv(g, 2)
                if after:
                    mixer_norm_group(*after)
                if here:
                    silu_conv(g, 3)
                if after:
                    act.wait_ge(m_win, (g + 1) * FC)
                    x_high(mixer_norm(after[0]), xt[0])

            split_high(0)
            split_high(1)
            act.wait_ge(s_whole, 16)
            act.activation(down_s[:], down_s[:], ACT.Copy, scale=0.5).then_inc(s_half_w, 1)
            norm_group(0, 0, 0)
            make_base(0, 0, 0, 0)
            x_high(0, xt[0])
            for i in range(2, len(loads)):
                split_high(i)
            act.wait_ge(s_small, 64)
            act.wait_ge(s_zero, 2)
            all_groups(act, route_groups)
            tiles(0)
            act.wait_ge(c_up, TILES)
            act.wait_ge(c_hid, TILES)
            act.wait_ge(c_xt, TILES)
            mixer_norm_group(0, 0, 0)
            x_high(NG, xt[0])
            all_groups(act, mix_groups)
            mix_groups(NG, NP, 0)
            tiles(1)

        @block.tensor
        def _(pe):
            def turn(m, src, free):
                pe.wait_ge(s_norm, m + 1)
                wait(pe, s_xthi, m)
                wait(pe, s_xtlo, m)
                free()
                for k in range(KC):
                    for i in range(G):
                        last = pe.transpose(pT[:, k, i * P:(i + 1) * P], src[:, i, k * P:(k + 1) * P], ident[:])
                last.then_inc(s_xt, 1)

            def cols(pair, at, n):
                return tuple(t[:, at:at + n] for t in pair)

            def project(out_ap, k_operands):
                products = [ab for s, m in k_operands for ab in split3(s, m)]
                for c, (s, m) in enumerate(products):
                    last = pe.matmul(out_ap, s, m, start=(c == 0), stop=(c == len(products) - 1))
                return last

            def gate_logits(n, m, x):
                pe.wait_ge(s_xthi, m + 1)
                pe.wait_ge(s_xtlo, m + 1)
                wait(pe, s_logit, n)
                for i in range(G):
                    last = project(p_gate[:, i, :], [(cols(x, k * GT + i * P, P), cols(gate, k * E, E))
                                                     for k in range(KC)])
                last.then_inc(s_gate, 1)

            def shared_up(n, x):
                wait(pe, s_ranked, n)
                wait(pe, s_hid, n)
                for h in range(2):
                    last = project(p_up[h], [(cols(up_s, k * HU + h * H, H), cols(x, k * GT, GT))
                                             for k in range(KC)])
                last.then_inc(s_up, 1)

            def ranks(n):
                pe.wait_ge(s_members, n + 1)
                pe.wait_ge(s_silu, n + 1)
                for i in range(G):
                    for c in range(i + 1):
                        pe.matmul(p_rank[:, i, :], (before if c == 0 else ones)[:],
                                  members[:, i if c == 0 else c - 1, :], start=(c == 0), stop=(c == i))
                for i in range(G):
                    last = pe.matmul(p_total, ones[:], members[:, i, :], start=(i == 0), stop=(i == G - 1))
                last.then_inc(s_rank, 1)

            def down(n, dst):
                pe.wait_ge(s_hid, n + 1)
                for i in range(G):
                    last = pe.matmul(dst[:, i // 2, (i % 2) * D:(i % 2 + 1) * D], hid[:, i * P:(i + 1) * P],
                                     down_s[:], start=True, stop=True)
                last.then_inc(s_down, 1)

            def route_groups(g, j, b):
                _, after = neighbours(g, j, b)
                gate_logits(g, g, xt[b])
                shared_up(g, xt[b])
                if after:
                    turn(after[0], norm[after[2]], lambda: pe.wait_ge(s_logit, g + 1))
                ranks(g)
                wait(pe, s_sum, g)
                down(g, pO)

            def tiles(f):
                pe.wait_ge(s_hid, NG * (f + 1))
                pe.wait_ge(s_ranked, NG * (f + 1))
                pe.wait_ge(s_sum, NG * (f + 1))
                pe.wait_ge(s_tabd, 32 * (f + 1))
                pe.wait_ge(s_whi, WEIGHTS)
                pe.wait_ge(s_wlo, WEIGHTS)
                pe.wait_ge(s_list, 32 * (f + 1))
                for h in range(2):
                    last = pe.transpose(p_lists[:, h * P:(h + 1) * P], list_rows[:, h, :], ident[:])
                last.then_inc(s_listt, 1)
                pe.wait_ge(s_tokens, f + 1)
                words = {}
                held = pe.alloc_register(f"experts_word{f}")

                def step(u, q, i):
                    done = f * TILES
                    if i == 0:
                        words.clear()
                    if tile := back(u, q, i, 0):
                        t, round_, r = tile
                        pe.wait_ge(c_in[r], (round_ + f * NQ + 1) * 16)
                        wait(pe, c_hi, t + done - 1)
                        wait(pe, c_lo, t + done - 1)
                        for k in range(KC):
                            last = pe.transpose(pT[:, r % 2, k * P:(k + 1) * P],
                                                tile_in[r % BUFS][:, k * P:(k + 1) * P], ident[:])
                        last.then_inc(c_xt, 1)
                    if tile := back(u, q, i, UP_LAG):
                        t, _, r = tile
                        e = expert_in(words, q, (i - UP_LAG) // RING, r)
                        pe.wait_ge(c_hi, t + done + 1)
                        pe.wait_ge(c_lo, t + done + 1)
                        wait(pe, c_hid, t + done - 1)
                        last = project(p_tile_up[r % 2],
                                       [(cols(tile_x[r % 2], k * P, P),
                                         tuple(w[:, bass.ds(e * (KC * HU) + k * HU, HU)] for w in up_e))
                                        for k in range(KC)])
                        last.then_inc(c_up, 1)
                    if tile := back(u, q, i, HT_LAG):
                        t, _, r = tile
                        pe.wait_ge(c_hid, t + done + 1)
                        wait(pe, c_hidhi, t + done - 1)
                        wait(pe, c_hidlo, t + done - 1)
                        pe.transpose(p_tile_ht[r % 2], tile_hid[r % 2], ident[:]).then_inc(c_ht, 1)
                    if tile := back(u, q, i, DOWN_LAG):
                        t, _, r = tile
                        e = expert_in(words, q, (i - DOWN_LAG) // RING, r)
                        pe.wait_ge(c_hidhi, t + done + 1)
                        pe.wait_ge(c_hidlo, t + done + 1)
                        wait(pe, c_out, t + done - 1)
                        last = project(pO[:, r % 2, 0:D],
                                       [(tile_hidp[r % 2], tuple(w[:, bass.ds(e * D, D)] for w in down_e))])
                        last.then_inc(c_down, 1)

                def expert_in(words, q, offset, r):
                    key = (offset, r // PACK)
                    if key not in words:
                        if offset == 0:
                            at = q * (RING // PACK) + r // PACK
                            pe.reg_load(held, tab_row[0:1, bass.ds(at, 1)])
                        words[key] = pe.snap(held, min_val=0, max_val=E ** PACK - 1)
                    return (words[key] // (E ** (r % PACK))) % E

                all_tiles(pe, step, DOWN_LAG)

            def w_in_chunk(g, f):
                c = g * FC
                if f == 0:
                    wait(pe, s_hid, g + NG - 1)
                    wait(pe, m_tap0, c)
                elif f == 1:
                    pe.wait_ge(s_ranked, g + NG - 1)
                    wait(pe, m_sz, c)
                elif f == 2:
                    pe.wait_ge(m_tap0, c + 1)
                    pe.wait_ge(m_sz, c + 1)
                else:
                    pe.wait_ge(m_sz, c + 3)
                for h in range(2):
                    last = project(p_mix[f][h], [(cols(win, k * 2 * M + h * M + f * P, P), cols(xt[0], k * GT, GT))
                                                 for k in range(KC)])
                last.then_inc(m_win, 1)

            def w_out_chunk(g, f):
                if f == 0:
                    wait(pe, m_x3, g)
                pe.wait_ge(m_mix, g * FC + f + 1)
                for i in range(G):
                    last = pe.matmul(pO[:, i // 2, (i % 2) * D:(i % 2 + 1) * D], conv[f][:, i * P:(i + 1) * P],
                                     wout[:, f * D:(f + 1) * D], start=(f == 0 and i % 2 == 0),
                                     stop=(f == FC - 1), skip_group_check=True)
                last.then_inc(m_wout, 1)

            def mix_groups(g, j, b):
                prev, after = neighbours(g, j, b)
                here = not (isinstance(g, int) and g >= NG)
                if here:
                    pe.wait_ge(s_xthi, mixer_norm(g) + 1)
                    pe.wait_ge(s_xtlo, mixer_norm(g) + 1)
                    w_in_chunk(g, 0)
                    w_in_chunk(g, 1)
                    w_in_chunk(g, 2)
                if prev:
                    turn(ffn_norm(prev[0]), norm[1], lambda: wait(pe, s_sum, g + NG - 1))
                if here:
                    w_in_chunk(g, 3)
                if prev:
                    gate_logits(prev[0] + NG, ffn_norm(prev[0]), xt[1])
                    if here:
                        pe.wait_ge(m_tap0, g * FC + 3)
                        pe.wait_ge(m_sz, g * FC + 2)
                    shared_up(prev[0] + NG, xt[1])
                if here:
                    w_out_chunk(g, 0)
                    w_out_chunk(g, 1)
                if prev:
                    ranks(prev[0] + NG)
                    down(prev[0] + NG, pT)
                if after:
                    turn(mixer_norm(after[0]), norm[0], lambda: wait(pe, s_sum, g + NG))
                if here:
                    w_out_chunk(g, 2)
                    w_out_chunk(g, 3)

            pe.wait_ge(s_const, CONSTS)
            turn(0, norm[0], lambda: None)
            pe.wait_ge(s_whi, LOADS_A)
            pe.wait_ge(s_wlo, LOADS_A)
            pe.wait_ge(s_half_w, 1)
            all_groups(pe, route_groups)
            tiles(0)
            pe.wait_ge(c_out, TILES)
            pe.wait_ge(s_small, 64)
            turn(NG, norm[0], lambda: None)
            all_groups(pe, mix_groups)
            mix_groups(NG, NP, 0)
            tiles(1)

        @block.vector
        def _(dve):
            def split_low(i):
                pair, at, cols, scale, _ = loads[i]
                dve.wait_ge(s_whi, i + 1)
                dve.scalar_tensor_tensor(pair[1][:, at:at + cols], stage[i % 2][:, 0:cols], scale,
                                         pair[0][:, at:at + cols], ALU.mult, ALU.subtract).then_inc(s_wlo, 1)

            def split_low_experts(j, b):
                dve.wait_ge(s_whi, j * 2 + b + len(loads) + 1)
                dst, cols, scale = ((up_e, UP2, 1.0), (down_e, DOWN2, 0.5))[b]
                dve.scalar_tensor_tensor(dst[1][:, bass.ds(j * cols, cols)], stage[b][:, 0:cols], scale,
                                         dst[0][:, bass.ds(j * cols, cols)], ALU.mult, ALU.subtract)\
                   .then_inc(s_wlo, 1)

            def statistics(m, src):
                wait(dve, s_norm, m)
                for i in range(G):
                    last = dve.bn_stats(stats[:, i, :], src[:, i, :])
                last.then_inc(s_stats, 1)
                dve.wait_ge(s_stats, m + 1)
                dve.sem_inc(s_passed_dve, 1)
                for i in range(G):
                    last = dve.bn_aggr(mean_var[:, i, :], stats[:, i, :])
                last.then_inc(s_aggr, 1)
                dve.wait_ge(s_aggr, m + 1)
                dve.tensor_scalar(var_eps[:], mean_var[:, :, 1], EPS, None, ALU.add).then_inc(s_vareps, 1)

            def affine(m, n=None):
                dve.wait_ge(s_rstd, m + 1)
                last = dve.scalar_tensor_tensor(norm_shift[:], mean_var[:, :, 0], -1.0, rstd[:], ALU.mult, ALU.mult)
                if n is not None:
                    wait(dve, s_base, n)
                    dve.tensor_scalar(base_scale[:], rstd[:], 0.5, 1.0, ALU.mult, ALU.add)
                    last = dve.scalar_tensor_tensor(base_shift[:], mean_var[:, :, 0], -0.5, rstd[:],
                                                    ALU.mult, ALU.mult)
                last.then_inc(s_shift, 1)

            def x_low(m, dst):
                dve.wait_ge(s_xthi, m + 1)
                for k in range(KC):
                    last = dve.tensor_tensor(dst[1][:, k * GT:(k + 1) * GT], pT[:, k, :],
                                             dst[0][:, k * GT:(k + 1) * GT], ALU.subtract)
                last.then_inc(s_xtlo, 1)

            def choose(f, g):
                n = g + f * NG
                k = [0]

                def then(ins):
                    k[0] += 1
                    ins.then_inc(s_route, 1)
                    dve.wait_ge(s_route, n * (CHOOSE_STEPS + PLACE_STEPS) + k[0])

                dve.wait_ge(s_gate, n + 1)
                dve.tensor_tensor(logit[:], p_gate, gate_bias[:].unsqueeze(1).to_broadcast([P, G, E]), ALU.add)\
                   .then_inc(s_logit, 1)
                dve.wait_ge(s_logit, n + 1)
                then(dve.tensor_scalar(logit[:], logit[:], SATURATED, None, ALU.min))
                dve.sem_inc(s_passed_dve, 1)
                for i in range(G):
                    last = dve.max(best[:, i, :], logit[:, i, :])
                then(last)
                dve.sem_inc(s_passed_dve, 1)
                for i in range(G):
                    last = dve.max_index(best_at[:, i, :], best[:, i, :], logit[:, i, :])
                then(last)
                dve.tensor_copy(logit_of[:, bass.ds(g * G * K, G * K)].rearrange("p (i k) -> p i k", k=K),
                                best[:, :, 0:K])
                then(dve.tensor_copy(chosen[:].rearrange("p (i k) -> p i k", k=K), best_at[:, :, 0:K]))
                then(dve.tensor_tensor(onehot[:], chosen[:].unsqueeze(2).to_broadcast([P, G * K, E]),
                                       expert_ids[:].unsqueeze(1).to_broadcast([P, G * K, E]), ALU.is_equal))
                wait(dve, s_rank, n)
                dve.tensor_tensor(members[:], onehot[:, 0::K, :], onehot[:, 1::K, :], ALU.add).then_inc(s_members, 1)
                dve.tensor_copy(expert_of[:, bass.ds(g * G * K, G * K)], chosen[:])
                assert k[0] == CHOOSE_STEPS

            def place(f, g, j, b):
                n = g + f * NG
                k = [CHOOSE_STEPS]

                def then(ins):
                    k[0] += 1
                    ins.then_inc(s_route, 1)
                    dve.wait_ge(s_route, n * (CHOOSE_STEPS + PLACE_STEPS) + k[0])

                dve.wait_ge(s_rank, n + 1)
                then(dve.tensor_tensor(rank_all[:], p_rank, counts[:, f, :].unsqueeze(1).to_broadcast([P, G, E]),
                                       ALU.add))
                dve.tensor_tensor(counts[:, f, :], counts[:, f, :], p_total, ALU.add).then_inc(s_ranked, 1)
                then(dve.tensor_tensor(rank_pick[:].rearrange("p (i k) e -> p i k e", k=K),
                                       onehot[:].rearrange("p (i k) e -> p i k e", k=K),
                                       rank_all[:].unsqueeze(2).to_broadcast([P, G, K, E]), ALU.mult))
                then(dve.tensor_reduce(rank[:], rank_pick[:], AX.X, ALU.add))
                dve.tensor_copy(rank_of[:, bass.ds(g * G * K, G * K)], rank[:])
                wait(dve, s_scat[b], (j + f * NP) * SCAT)
                dve.scalar_tensor_tensor(slot[b][:], chosen[:], float(T), rank[:], ALU.mult, ALU.add)\
                   .then_inc(s_slot, 1)
                assert k[0] == CHOOSE_STEPS + PLACE_STEPS

            CHOOSE_STEPS, PLACE_STEPS = 5, 3

            def shared_hidden(n):
                dve.wait_ge(s_silu, n + 1)
                wait(dve, s_down, n)
                dve.tensor_tensor(hid[:], silu_g[:], p_up[1], ALU.mult).then_inc(s_hid, 1)

            def make_sum(n, b, src):
                dve.wait_ge(s_down, n + 1)
                dve.wait_ge(s_base, n + 1)
                for h in range(2):
                    half = base[b][:, 2 * h:2 * h + 2, :].rearrange("p i d -> p (i d)")
                    last = dve.tensor_tensor(half, src[:, h, :], half, ALU.add)
                last.then_inc(s_sum, 1)

            def start_norm(g, j, b):
                dve.wait_ge(s_rows[b], (j + 1) * 16)
                statistics(g, rows[b])

            def route_groups(g, j, b):
                _, after = neighbours(g, j, b)
                if after:
                    affine(after[0], after[0])
                choose(0, g)
                shared_hidden(g)
                place(0, g, j, b)
                if after:
                    x_low(after[0], xt[after[2]])
                if not (isinstance(g, int) and g >= NG - 2):
                    start_norm(g + 2, j + 1, b)
                split_low_experts(j, b)
                make_sum(g, b, pO)

            def plan(f):
                k = [0]

                def then(ins):
                    k[0] += 1
                    ins.then_inc(s_plan, 1)
                    dve.wait_ge(s_plan, f * PLAN_STEPS + k[0])

                dve.wait_ge(s_ranked, NG * (f + 1))
                then(dve.tensor_scalar(tiles_i[:], counts[:, f, :], float(P - 1), None, ALU.add))
                then(dve.tensor_scalar(tiles_i[:], tiles_i[:], P.bit_length() - 1, None, ALU.logical_shift_right))
                then(dve.tensor_copy(tiles_f[:], tiles_i[:]))
                then(dve.tensor_tensor_scan(tiles_upto[:], ones_e[:], tiles_f[:], 0.0, ALU.mult, ALU.add))
                then(dve.tensor_tensor(passed[:], tile_ids[:].unsqueeze(2).to_broadcast([P, PACK + 2, E]),
                                       tiles_upto[:].unsqueeze(1).to_broadcast([P, PACK + 2, E]), ALU.is_ge))
                then(dve.tensor_tensor(passed_n[:], passed[:], tiles_f[:].unsqueeze(1).to_broadcast([P, PACK + 2, E]),
                                       ALU.mult))
                dve.tensor_reduce(tab_e[:], passed[:], AX.X, ALU.add)
                then(dve.tensor_reduce(tab_s[:], passed_n[:], AX.X, ALU.add))
                then(dve.tensor_scalar(tab_e[:], tab_e[:], float(E - 1), None, ALU.min))
                then(dve.tensor_tensor(tab_s[:], tile_ids[:], tab_s[:], ALU.subtract))
                then(dve.scalar_tensor_tensor(tab_s[:], tab_e[:], float(COLS), tab_s[:], ALU.mult, ALU.add))
                wait(dve, s_list, 32 * f)
                dve.tensor_scalar(list_at[:], tab_s[:, PACK:PACK + 2], float(E * COLS - 1), None, ALU.min)\
                   .then_inc(s_listat, 1)
                for c in range(PACK - 2, -1, -1):
                    high = tab_e[:, PACK - 1:PACK] if c == PACK - 2 else tab_pack[:, c + 1:c + 2]
                    then(dve.scalar_tensor_tensor(tab_pack[:, c:c + 1], high, float(E), tab_e[:, c:c + 1],
                                                  ALU.mult, ALU.add))
                wait(dve, s_tabd, 32 * f)
                dve.tensor_copy(tab_i[:], tab_pack[:, 0:1]).then_inc(s_tab, 1)
                then(dve.tensor_tensor(first_row[:], tiles_upto[:], tiles_f[:], ALU.subtract))
                then(dve.tensor_scalar(first_row[:], first_row[:], float(P), None, ALU.mult))
                wide = rows[0][:].rearrange("p i (c e) -> p (i c) e", e=E)
                half = NT * K // 2
                dve.wait_ge(s_base, NG * (f + 1))
                for h in range(2):
                    part = slice(h * half, (h + 1) * half)
                    then(dve.tensor_tensor(wide, expert_of[:, part].unsqueeze(2).to_broadcast([P, half, E]),
                                           expert_ids[:].unsqueeze(1).to_broadcast([P, half, E]), ALU.is_equal))
                    then(dve.tensor_tensor(wide, wide, first_row[:].unsqueeze(1).to_broadcast([P, half, E]),
                                           ALU.mult))
                    then(dve.tensor_reduce(expert_of[:, part], wide, AX.X, ALU.add))
                then(dve.tensor_tensor(position[:], expert_of[:], rank_of[:], ALU.add))
                dve.wait_ge(s_exp, f + 1)
                then(dve.tensor_scalar(exp_neg, exp_neg, 1.0, None, ALU.add))
                then(dve.tensor_tensor(denom[:], exp_neg[:, :, 0], exp_neg[:, :, 1], ALU.add))
                then(dve.reciprocal(denom[:], denom[:]))
                dve.tensor_tensor(weight[:, :, 0], exp_neg[:, :, 1], denom[:], ALU.mult)
                dve.tensor_tensor(weight[:, :, 1], exp_neg[:, :, 0], denom[:], ALU.mult).then_inc(s_pos, 1)
                assert k[0] == PLAN_STEPS

            PLAN_STEPS = 27

            def tiles(f):
                dve.wait_ge(s_down, NG * (f + 1))

                def step(u, q, i):
                    done = f * TILES
                    if tile := back(u, q, i, 0):
                        t, _, r = tile
                        dve.wait_ge(c_hi, t + done + 1)
                        dve.tensor_tensor(tile_x[r % 2][1], pT[:, r % 2, 0:D], tile_x[r % 2][0], ALU.subtract)\
                           .then_inc(c_lo, 1)
                    if tile := back(u, q, i, UP_LAG):
                        t, _, r = tile
                        dve.wait_ge(c_silu, t + done + 1)
                        wait(dve, c_ht, t + done - 1)
                        dve.tensor_tensor(tile_hid[r % 2], tile_silu[r % 2], p_tile_up[r % 2][:, H:HU], ALU.mult)\
                           .then_inc(c_hid, 1)
                    if tile := back(u, q, i, HT_LAG):
                        t, _, r = tile
                        dve.wait_ge(c_hidhi, t + done + 1)
                        dve.tensor_tensor(tile_hidp[r % 2][1], p_tile_ht[r % 2], tile_hidp[r % 2][0], ALU.subtract)\
                           .then_inc(c_hidlo, 1)

                all_tiles(dve, step, HT_LAG)

            def combine(f, g, j, b):
                so_far = rows[b] if f else sum_in
                n = g + f * NG
                wait(dve, m_comb, n)
                dve.tensor_copy(weight_now[:].rearrange("p (i k) -> p i k", k=K), weight[:, bass.ds(g * G, G), :])\
                   .then_inc(m_weight, 1)
                dve.wait_ge(s_rows[b], (j + (f + 1) * NP + 1) * 16)
                dve.wait_ge(m_picked[b], (j + f * NP + 1) * SCAT)
                dve.wait_ge(m_weight, n + 1)
                if f == 0:
                    dve.wait_ge(s_base, NG if isinstance(g, int) and g == 0 else g + NG - 1)
                for k in range(K):
                    for i in range(G):
                        last = dve.scalar_tensor_tensor(rows[b][:, i, :], picked_in[b * f][i][k],
                                                        weight_now[:, i * K + k:i * K + k + 1],
                                                        (rows[b] if k else so_far)[:, i, :], ALU.mult, ALU.add)
                    last.then_inc(m_add if k == 0 else m_comb, 1)
                    if k == 0:
                        dve.wait_ge(m_add, n + 1)

            def start_mixer(g, j, b):
                combine(0, g, j, b)
                dve.wait_ge(m_comb, g + 1)
                statistics(mixer_norm(g), rows[b])

            def other_taps(g, f):
                c = g * FC + f
                dve.wait_ge(m_tap0, c + 1)
                for k in range(T3):
                    if k:
                        dve.wait_ge(m_tap, c * T3 + k)
                    dve.scalar_tensor_tensor(conv[f][:], xc[f % 2][:, k:k + GT], taps[:, f, k:k + 1], conv[f][:],
                                             ALU.mult, ALU.add).then_inc(m_tap, 1)

            def mix(g, f):
                c = g * FC + f
                dve.wait_ge(m_xa, c + 1)
                dve.wait_ge(m_sz, c + 1)
                dve.tensor_tensor(conv[f][:], conv[f][:], silu_z[f % 2][:], ALU.mult).then_inc(m_mix, 1)

            def end_mixer(g, b):
                dve.wait_ge(m_wout, (g + 1) * FC)
                for h in range(2):
                    half = rows[b][:, 2 * h:2 * h + 2, :].rearrange("p i d -> p (i d)")
                    last = dve.tensor_tensor(half, pO[:, h, :], half, ALU.add)
                last.then_inc(m_x3, 1)
                dve.wait_ge(m_x3, g + 1)

            def mix_groups(g, j, b):
                prev, after = neighbours(g, j, b)
                here = not (isinstance(g, int) and g >= NG)
                if prev:
                    pg, pj, pb = prev
                    end_mixer(pg, pb)
                    statistics(ffn_norm(pg), rows[pb])
                if here:
                    other_taps(g, 0)
                if prev:
                    affine(ffn_norm(pg), pg + NG)
                if here:
                    other_taps(g, 1)
                    mix(g, 0)
                    other_taps(g, 2)
                if prev:
                    x_low(ffn_norm(pg), xt[1])
                if here:
                    mix(g, 1)
                if after:
                    start_mixer(*after)
                if prev:
                    choose(1, pg)
                if after:
                    affine(mixer_norm(after[0]))
                if prev:
                    shared_hidden(pg + NG)
                if here:
                    other_taps(g, 3)
                    mix(g, 2)
                if prev:
                    make_sum(pg + NG, pb, pT)
                    place(1, *prev)
                if here:
                    mix(g, 3)
                if after:
                    x_low(mixer_norm(after[0]), xt[0])

            dve.memset(no_halo[:], 0.0).then_inc(s_zero, 1)
            dve.memset(counts[:], 0.0).then_inc(s_zero, 1)
            dve.wait_ge(s_zero, 2)
            start_norm(0, 0, 0)
            split_low(0)
            split_low(1)
            affine(0, 0)
            x_low(0, xt[0])
            for i in range(2, len(loads)):
                split_low(i)
            start_norm(1, 0, 1)
            dve.wait_ge(s_const, CONSTS)
            dve.wait_ge(s_small, 64)
            all_groups(dve, route_groups)
            plan(0)
            tiles(0)
            dve.wait_ge(c_xt, TILES)
            dve.wait_ge(c_ht, TILES)
            start_mixer(0, 0, 0)
            affine(NG)
            x_low(NG, xt[0])
            all_groups(dve, mix_groups)
            mix_groups(NG, NP, 0)
            plan(1)
            tiles(1)
            dve.wait_ge(c_xt, 2 * TILES)
            all_groups(dve, lambda g, j, b: combine(1, g, j, b))


_INS = ["x", "w_in", "w_conv", "b_conv", "w_out"]
_FFN = ["gate_w", "gate_b", "shared_wg", "shared_wu", "shared_wd", "experts_wg", "experts_wu", "experts_wd"]


def kernel(**inputs):
    import numpy as np
    import concourse.bacc as bacc
    from concourse.bass_utils import run_bass_kernel_spmd

    nc = bacc.Bacc("TRN2", target_bir_lowering=False, num_devices=1)
    arrays, args = {}, []
    for name in [f"L0_attn_{n}" for n in _INS] + [f"L0_ffn_{n}" for n in _FFN]:
        a = np.ascontiguousarray(inputs[name])
        arrays[f"in_{name}"] = a
        args.append(nc.dram_tensor(f"in_{name}", a.shape, mybir.dt.from_np(a.dtype), kind="ExternalInput").ap())
    shape = inputs["L0_attn_x"].shape
    args.append(nc.dram_tensor("out_0", shape, F32, kind="ExternalOutput").ap())
    build_macaron(nc, *args)
    r = run_bass_kernel_spmd(nc, [arrays], core_ids=[0])
    return r.results[0]["out_0"]
```
